# Optimizing a Trainium2 kernel written in Bass

```python
import numpy as np
import jax
import jax.numpy as jnp

def _softmax(x, axis=-1):
    return jax.nn.softmax(x, axis=axis)

def _gelu(x):
    return jax.nn.gelu(x, approximate=True)

def _silu(x):
    return jax.nn.silu(x)

def _sigmoid(x):
    return jax.nn.sigmoid(x)

def _layernorm(x, axis=-1, eps=1e-05):
    m = jnp.mean(x, axis=axis, keepdims=True)
    v = jnp.var(x, axis=axis, keepdims=True)
    return (x - m) / jnp.sqrt(v + eps)

def _scatter_add(tgt, idx, src, axis=0):
    return tgt.at[idx].add(src)

def _segment_sum(src, seg, n):
    return jax.ops.segment_sum(src, seg, n)
kernel_name = 'mk_gnn_resnorm_d2_gnn_r64_3adfcb'

def setup_inputs(seed: int=0):
    np.random.seed(seed)
    _w = jnp.asarray

    def _rec_inputs():
        import jax
        import jax.numpy as jnp
        _gk = jax.random.key(seed)
        x = -0.0003929 + 0.9999 * jax.random.normal(jax.random.fold_in(_gk, 1), (256, 1024), jnp.float32)
        src = jax.random.randint(jax.random.fold_in(_gk, 2), (8192,), 0, 256, jnp.int32)
        dst = jax.random.randint(jax.random.fold_in(_gk, 3), (8192,), 0, 256, jnp.int32)
        _o = jnp.argsort(dst, stable=True)
        src = src[_o]
        dst = dst[_o]
        return (x, src, dst)
    x, src, dst = _rec_inputs()

    def _L0_gnn_setup():
        import jax, jax.numpy as jnp
        import numpy as np
        NH, NO = (64, 192)
        N = NH + NO
        E_HH, E_OO, E_HO = (128, 640, 256)
        E = E_HH + E_OO + E_HO
        D = 1024
        key = jax.random.key(seed)
        ks = jax.random.split(key, 12)
        w = lambda k, s: jax.random.normal(k, s, jnp.float32) * 0.02
        return {'n_f': jax.random.normal(ks[0], (N, D), jnp.float32), 'W_hh': w(ks[1], (2 * D, D)), 'b_hh': jnp.zeros((D,), jnp.float32), 'W_oo': w(ks[2], (2 * D, D)), 'b_oo': jnp.zeros((D,), jnp.float32), 'W_ho': w(ks[3], (2 * D, D)), 'b_ho': jnp.zeros((D,), jnp.float32), 'W_a': w(ks[4], (D, 1)), 'b_a': jnp.zeros((1,), jnp.float32), 'W_hn': w(ks[5], (2 * D, D)), 'b_hn': jnp.zeros((D,), jnp.float32), 'W_on': w(ks[6], (2 * D, D)), 'b_on': jnp.zeros((D,), jnp.float32), 'edge_src': jax.random.randint(ks[7], (E,), 0, N, jnp.int32), 'edge_dst': jax.random.randint(ks[8], (E,), 0, N, jnp.int32)}
    _L0_gnn_all = _L0_gnn_setup()
    _L0_gnn_in = {k: v for k, v in _L0_gnn_all.items() if k in ('W_hh', 'b_hh', 'W_oo', 'b_oo', 'W_ho', 'b_ho', 'W_a', 'b_a', 'W_hn', 'b_hn', 'W_on', 'b_on')}
    del _L0_gnn_all

    def _L1_gnn_setup():
        import jax, jax.numpy as jnp
        import numpy as np
        NEG_SLOPE = 0.1
        EPS = 1e-05
        key = jax.random.key(seed)
        k1, k2, k3, k4, k5 = jax.random.split(key, 5)
        N, E, DIN, DOUT = (10000, 2500, 1024, 1024)
        x = jax.random.normal(k1, (N, DIN), dtype=jnp.float32)
        W = jax.random.normal(k2, (DIN, DOUT), dtype=jnp.float32) * 0.02
        a = jax.random.normal(k3, (1, 2 * DOUT), dtype=jnp.float32) * 0.02
        src = jax.random.randint(k4, (E,), 0, N, dtype=jnp.int64)
        dst = jax.random.randint(k5, (E,), 0, N, dtype=jnp.int64)
        return {'x': x, 'W': W, 'a': a, 'src': src, 'dst': dst}
    _L1_gnn_all = _L1_gnn_setup()
    _L1_gnn_in = {k: v for k, v in _L1_gnn_all.items() if k in ('W', 'a')}
    del _L1_gnn_all
    return {'x': x, 'src': src, 'dst': dst, 'L0_gnn_W_hh': _L0_gnn_in['W_hh'], 'L0_gnn_b_hh': _L0_gnn_in['b_hh'], 'L0_gnn_W_oo': _L0_gnn_in['W_oo'], 'L0_gnn_b_oo': _L0_gnn_in['b_oo'], 'L0_gnn_W_ho': _L0_gnn_in['W_ho'], 'L0_gnn_b_ho': _L0_gnn_in['b_ho'], 'L0_gnn_W_a': _L0_gnn_in['W_a'], 'L0_gnn_b_a': _L0_gnn_in['b_a'], 'L0_gnn_W_hn': _L0_gnn_in['W_hn'], 'L0_gnn_b_hn': _L0_gnn_in['b_hn'], 'L0_gnn_W_on': _L0_gnn_in['W_on'], 'L0_gnn_b_on': _L0_gnn_in['b_on'], 'L1_gnn_W': _L1_gnn_in['W'], 'L1_gnn_a': _L1_gnn_in['a']}

def reference(x, src, dst, L0_gnn_W_hh, L0_gnn_b_hh, L0_gnn_W_oo, L0_gnn_b_oo, L0_gnn_W_ho, L0_gnn_b_ho, L0_gnn_W_a, L0_gnn_b_a, L0_gnn_W_hn, L0_gnn_b_hn, L0_gnn_W_on, L0_gnn_b_on, L1_gnn_W, L1_gnn_a):
    import jax
    import jax.numpy as jnp

    def _L0_gnn_ref(n_f, W_hh, b_hh, W_oo, b_oo, W_ho, b_ho, W_a, b_a, W_hn, b_hn, W_on, b_on, edge_src, edge_dst):
        import jax, jax.numpy as jnp
        import numpy as np
        NH, NO = (64, 192)
        N = NH + NO
        E_HH, E_OO, E_HO = (128, 640, 256)
        E = E_HH + E_OO + E_HO
        D = 1024
        feat = jnp.concatenate([n_f[edge_src], n_f[edge_dst]], axis=1)
        e_hh = jax.nn.relu(feat[:E_HH] @ W_hh + b_hh)
        e_oo = jax.nn.relu(feat[E_HH:E_HH + E_OO] @ W_oo + b_oo)
        e_ho = jax.nn.relu(feat[E_HH + E_OO:] @ W_ho + b_ho)
        e_f = jnp.concatenate([e_hh, e_oo, e_ho], axis=0)
        logit = (e_f @ W_a + b_a)[:, 0]
        m = jax.lax.stop_gradient(jax.ops.segment_max(logit, edge_dst, num_segments=N))
        ex = jnp.exp(logit - m[edge_dst])
        den = jax.ops.segment_sum(ex, edge_dst, num_segments=N)
        alpha = ex / den[edge_dst]
        z_f = jax.ops.segment_sum(alpha[:, None] * n_f[edge_src], edge_dst, num_segments=N)
        nf2 = jnp.concatenate([n_f, z_f], axis=1)
        h_new = jax.nn.relu(nf2[:NH] @ W_hn + b_hn)
        o_new = jax.nn.relu(nf2[NH:] @ W_on + b_on)
        return jnp.concatenate([h_new, o_new], axis=0)

    def _L1_gnn_ref(x, W, a, src, dst):
        import jax, jax.numpy as jnp
        import numpy as np
        NEG_SLOPE = 0.1
        EPS = 1e-05
        N = x.shape[0]
        d = W.shape[1]
        h = x @ W
        a_l, a_r = (a[0, :d], a[0, d:])
        al = h @ a_l
        ar = h @ a_r
        e = jnp.exp(-jax.nn.leaky_relu(al[src] + ar[dst], negative_slope=NEG_SLOPE))
        rowsum = jax.ops.segment_sum(e, src, num_segments=N)
        h_prime = jax.ops.segment_sum(e[:, None] * h[dst], src, num_segments=N)
        h_prime = h_prime / (rowsum[:, None] + EPS)
        return jax.nn.elu(h_prime)
    x = _layernorm(x + _L0_gnn_ref(x, L0_gnn_W_hh, L0_gnn_b_hh, L0_gnn_W_oo, L0_gnn_b_oo, L0_gnn_W_ho, L0_gnn_b_ho, L0_gnn_W_a, L0_gnn_b_a, L0_gnn_W_hn, L0_gnn_b_hn, L0_gnn_W_on, L0_gnn_b_on, src, dst), axis=-1)
    x = _layernorm(x + _L1_gnn_ref(x, L1_gnn_W, L1_gnn_a, src, dst), axis=-1)
    return x

_drawn_inputs = setup_inputs


def setup_inputs(seed=0):
    import zlib

    import numpy as np

    out = dict(_drawn_inputs(seed))
    spreads = {'L0_gnn_b_hh': (0.0, 2.0),
     'L0_gnn_b_oo': (0.0, 2.0),
     'L0_gnn_b_ho': (0.0, 0.8),
     'L0_gnn_b_hn': (0.0, 0.1),
     'L0_gnn_b_on': (0.0, 0.1)}
    factors = {'L0_gnn_W_hh': 8.0, 'L0_gnn_W_oo': 8.0, 'L0_gnn_W_ho': 2.998, 'L0_gnn_W_a': 2.766}
    for name, (base, spread) in spreads.items():
        noise = np.random.default_rng([zlib.crc32(name.encode()), seed]).standard_normal(out[name].shape)
        drawn = base * np.exp(spread * noise) if base else spread * noise
        out[name] = jnp.asarray(drawn.astype(out[name].dtype))
    for name, factor in factors.items():
        out[name] = (out[name] * factor).astype(out[name].dtype)
    return out
```

```python
from contextlib import ExitStack

import concourse.bass as bass
from concourse import mybir

P = 128
N = 256
D = 1024
E = 8192
NH = 64
E_HH, E_OO = 128, 640
E_ST = E_HH + E_OO
E_HO = E - E_ST
JH = E_HO // P
JO = E_OO // P
Q = 64
NC = (N // Q) ** 2
NT = JH + NC
NT += NT % 2
KC = D // P
NS = 6
SLOPE, EPS_L1, EPS_LN = 0.1, 1e-5, 1e-5
BIG = 3.0e38

F32 = mybir.dt.float32
F32R = mybir.dt.float32r
BF16 = mybir.dt.bfloat16
I32 = mybir.dt.int32
U8 = mybir.dt.uint8
ALU = mybir.AluOpType
ACT = mybir.ActivationFunctionType
AX = mybir.AxisListType.X


def gnn_two_layers(nc, x, src, dst, W_hh, b_hh, W_oo, b_oo, W_ho, b_ho, W_a, b_a, W_hn, b_hn, W_on, b_on,
                   L1_W, L1_a, out):
    ctx = ExitStack()
    with ctx:
        def sb(name, shape, dt=F32, stack=ctx):
            return stack.enter_context(nc.sbuf_tensor(name, shape, dt))

        def sem(name):
            return ctx.enter_context(nc.semaphore(name))

        x_nat = sb("x_nat", [P, 2, D])
        x_T = sb("x_T", [P, KC, N])
        W_ring = sb("W_ring", [P, NS, 2, D])
        A_tab = sb("A_tab", [P, 4, D], F32R)
        key_rows = sb("key_rows", [P, 2, NT * P], U8)
        wa_bc = sb("wa_bc", [P, D])
        bias_bc = sb("bias_bc", [P, 2, D])
        ident = sb("ident", [P, P])
        irow = sb("irow", [P, N + 1])
        pcol = sb("pcol", [P, 3])
        tri = sb("tri", [P, P], BF16)
        ones_b = sb("ones_b", [P, P], BF16)
        ones_f = sb("ones_f", [P, P])
        zero_r = sb("zero_r", [1, 512])
        spare = sb("spare", [1, 6])
        st_col = sb("st_col", [P, 2, 1 + JO], I32)
        st_colf = sb("st_colf", [P, 2, 1 + JO])
        key_col = sb("key_col", [P, 2, NT])
        dkey = sb("dkey", [P, NT])
        steer = sb("steer", [1, NT // 2 + 1, 8], I32)
        logit = sb("logit", [P, NT])
        st_logit = sb("st_logit", [P, 1 + JO])
        oh = sb("oh", [P, 2, 2, P], F32R)
        key_now = sb("key_now", [P, 2, 2 * P], U8)
        dkey_now = sb("dkey_now", [P, 2])
        sc_l = sb("sc_l", [P, 2, P])
        sc_r = sb("sc_r", [P, 2, 2, Q])
        junk = sb("junk", [P, D], BF16)
        small = sb("small", [P, 64])
        eps_ln = sb("eps_ln", [P, 1])
        ba_bc = sb("ba_bc", [P, 1])
        bnT = sb("bnT", [P, 2, KC])
        st_row = sb("st_row", [P, 2, E_ST], I32)

        key_dram = nc.dram_tensor("key_rows_scratch", [2, NT, P], U8, kind="Internal").ap()

        ps = ctx.enter_context(nc.psum_tensor("ps", [P, 4096], F32))
        G0, G1 = ps[:, 0:2048], ps[:, 2048:4096]

        x_in = sem("x_in")
        edges_in = sem("edges_in")
        st_rows_in = sem("st_rows_in")
        consts_in = sem("consts_in")
        biases_in = sem("biases_in")
        w_in = [sem(f"w_in{i}") for i in range(NS)]
        w_used = sem("w_used")
        pool_done = sem("pool_done")
        dve_done = sem("dve_done")
        setup_done = sem("setup_done")
        pe_step = sem("pe_step")
        act_step = sem("act_step")
        dve_step = sem("dve_step")
        keys_out = sem("keys_out")
        keys_back = sem("keys_back")
        st_oh = sem("st_oh")
        oh_made = sem("oh_made")
        keys_staged = sem("keys_staged")
        gathered = sem("gathered")
        reduced = sem("reduced")
        sc_made = sem("sc_made")
        scattered = sem("scattered")
        dl_made = sem("dl_made")
        out_in = sem("out_in")

        early = ExitStack()
        edges = sb("edges", [P, 2, JH], I32, early)
        eq_i = sb("eq_i", [P, 2, JH], I32, early)
        el_i = sb("el_i", [P, 2, JH], I32, early)
        cls = sb("cls", [P, JH], F32, early)
        val = sb("val", [P, 2, JH], BF16, early)
        cls_oh = sb("cls_oh", [P, NC, JH], F32, early)
        gate = sb("gate", [P, NC, JH], F32, early)
        cum = sb("cum", [P, NC, JH], F32, early)
        tot = sb("tot", [P, NC], BF16, early)
        cw = sb("cw", [P, 6, NC], F32, early)
        cwi = sb("cwi", [P, 2, NC], I32, early)
        slot = sb("slot", [P, JH], F32, early)
        slot_i = sb("slot_i", [P, 3, JH], I32, early)
        slot_f = sb("slot_f", [P, 2, JH], F32, early)
        pos_oh = sb("pos_oh", [P, JH, P], BF16, early)
        tile_val = sb("tile_val", [P, JH, 2, NT], BF16, early)
        cle = sb("cle", [P, NT, NC], BF16, early)
        tcls = sb("tcls", [P, 2, NT], F32, early)
        tcls_i = sb("tcls_i", [P, 5, NT], I32, early)
        key_u8 = sb("key_u8", [NT, 2, P], U8, early)
        early.close()
        S_log = sb("S_log", [P, 3, 2, N])
        S_cnt = sb("S_cnt", [P, 3, 2, N])
        late = ExitStack()
        B_tab = sb("B_tab", [P, 4, D], F32R, late)
        Ao_tab = sb("Ao_tab", [P, 2, 2, D], F32R, late)
        Bo_tab = sb("Bo_tab", [P, 2, 2, D], F32R, late)
        hh_T = sb("hh_T", [P, 2, KC, P], F32, late)
        st_ohT = sb("st_ohT", [P, 2, 2, P], F32, late)
        st_ohTr = sb("st_ohTr", [P, 2, 2, P], F32R, late)
        st_scl = sb("st_scl", [P, N], F32, late)
        st_scr = sb("st_scr", [P, 2, N], F32, late)
        late.close()
        last = ExitStack()
        PT = sb("PT", [P, 2, N], F32, last)
        z_T = sb("z_T", [P, KC, N], F32, last)
        o_T = sb("o_T", [P, KC, N], F32, last)
        x1 = sb("x1", [P, 2, D], F32, last)
        h1 = sb("h1", [P, 2, D], F32, last)
        y1 = sb("y1", [P, 2, D], F32, last)
        y2 = sb("y2", [P, 2, D], F32, last)
        last.close()

        stream = []
        for name, W in (("ho", W_ho), ("oo", W_oo), ("hh", W_hh)):
            for k in range(0, 2 * KC, 2):
                stream.append(((name, k), W[k * P:(k + 2) * P, :]))
        for k in range(0, 2 * KC, 2):
            stream.append((("hn", k), W_hn[k * P:(k + 2) * P, :]))
            stream.append((("on", k), W_on[k * P:(k + 2) * P, :]))
        for k in range(0, KC, 2):
            stream.append((("l1", k), L1_W[k * P:(k + 2) * P, :]))
        turn = {key: n for n, (key, _) in enumerate(stream)}

        def chunk(name, k):
            return W_ring[:, turn[name, k - k % 2] % NS, k % 2, :]

        def w_arrived(eng, name, k):
            n = turn[name, k - k % 2]
            eng.wait_ge(w_in[n % NS], 16 * (n // NS + 1))

        PE_STAGES = ["xT", "totals", "perm", "keysT", "ghT", "PT", "zT", "nat", "x1T", "albc", "hp"]
        PAIRS = {"hoA": 4, "hoB": 8, "ooA": 12, "ooB": 16, "hh": 24, "upd": 40, "h1": 44}
        ACT_STAGES = ["xT", "hoA_hi", "hoB_hi", "ghT", "ooA_hi", "ooB_hi", "soft", "zT", "upd", "sd0", "x1T",
                      "h1", "lrelu", "elu", "sd1"]
        DVE_STAGES = ["tot", "perm_in", "key_col", "key_u8", "steer", "hoA_lo", "hoB_b", "hoB_lo", "ooA_lo", "ooB_b",
                      "ooB_lo", "D_hh", "D_oo", "D_ho", "masked", "P", "PT", "res0", "var0", "x1", "al", "lr",
                      "ET", "hpn", "res1", "var1", "out"]

        def pe_at(s):
            return PE_STAGES.index(s) + 1

        def act_at(s):
            return ACT_STAGES.index(s) + 1

        def dve_at(s):
            return DVE_STAGES.index(s) + 1

        block = ctx.enter_context(nc.Block())

        @block.sync
        def _(sp):
            sp.dma_start(x_nat[:], x.rearrange("(h p) d -> p h d", p=P)).then_inc(x_in, 16)
            for n, (_, rows) in enumerate(stream):
                if n >= NS:
                    sp.wait_ge(w_used, n - NS + 1)
                sp.dma_start(W_ring[:, n % NS, :, :], rows.rearrange("(i p) d -> p i d", p=P)) \
                  .then_inc(w_in[n % NS], 16)
                if n == len(stream) - 1:
                    sp.wait_ge(dve_step, dve_at("D_oo"))
                    sp.dma_start(bias_bc[:, 0, :], L1_a[0, 0:D].partition_broadcast(P)).then_inc(biases_in, 16)
                    sp.dma_start(bias_bc[:, 1, :], L1_a[0, D:2 * D].partition_broadcast(P)).then_inc(biases_in, 16)
            sp.wait_ge(dve_step, dve_at("out"))
            sp.dma_start(out.rearrange("(h p) d -> p h d", p=P), y2[:]).then_inc(out_in, 16)
            sp.wait_ge(out_in, 16)

        @block.gpsimd
        def _(pool):
            mine = [0]

            def link(ins):
                mine[0] += 1
                ins.then_inc(pool_done, 1)
                pool.wait_ge(pool_done, mine[0])

            ga = nc.gpsimd
            ga.memset(ident[:], 0.0).then_inc(pool_done, 1)
            ga.memset(tri[:], 1.0).then_inc(pool_done, 1)
            ga.memset(ones_b[:], 1.0).then_inc(pool_done, 1)
            ga.memset(ones_f[:], 1.0).then_inc(pool_done, 1)
            ga.memset(zero_r[:], 0.0).then_inc(pool_done, 1)
            ga.memset(gate[:], 1.0).then_inc(pool_done, 1)
            ga.memset(eps_ln[:], EPS_LN).then_inc(pool_done, 1)
            ga.iota(irow[:], pattern=[[1, N + 1]], base=0, channel_multiplier=0,
                    allow_small_or_imprecise_dtypes=True).then_inc(pool_done, 1)
            for h in range(2):
                ga.iota(pcol[:, 1 + h:2 + h], pattern=[[0, 1]], base=h * P, channel_multiplier=1,
                        allow_small_or_imprecise_dtypes=True).then_inc(pool_done, 1)
            pool.wait_ge(pool_done, 10)
            mine[0] = 10
            for q in range(2):
                link(ga.iota(pcol[q * Q:(q + 1) * Q, 0:1], pattern=[[0, 1]], base=1, channel_multiplier=1,
                             allow_small_or_imprecise_dtypes=True))
            link(ga.affine_select(out=ident[:], in_=ident[:], compare_op=ALU.not_equal, fill=1.0, base=0,
                                  pattern=[[-1, P]], channel_multiplier=1))
            link(ga.affine_select(out=tri[:], in_=tri[:], compare_op=ALU.is_gt, fill=0.0, base=0,
                                  pattern=[[1, P]], channel_multiplier=-1))
            link(ga.memset(gate[:, :, 0:1], 0.0))
            ga.nop().then_inc(setup_done, 1)

            pool.wait_ge(st_rows_in, 32)
            pool.wait_ge(dve_step, dve_at("steer"))
            pool.wait_ge(pe_step, pe_at("perm"))
            for k in range(2):
                for h in range(2):
                    ga.tensor_scalar(st_ohT[:, k, h, :], st_row[:, k, 0:P], pcol[:, 1 + h:2 + h], None,
                                     ALU.is_equal).then_inc(st_oh, 1)
            for t in range(JO):
                if t >= 1:
                    pool.wait_ge(gathered, t)
                for k in range(2):
                    v = st_row[:, k, E_HH:E_ST].rearrange("p (m t) -> p t m", t=JO)[:, t, :]
                    for h in range(2):
                        ga.tensor_scalar(st_ohTr[:, k, h, :], v, pcol[:, 1 + h:2 + h], None,
                                         ALU.is_equal).then_inc(st_oh, 1)

            def stage_keys(i):
                c = 2 * i * P if isinstance(i, int) else bass.ds(2 * i * P, 2 * P)
                d = 2 * i if isinstance(i, int) else bass.ds(2 * i, 2)
                ga.tensor_copy(key_now[:], key_rows[:, :, 0:2 * P] if isinstance(i, int) else key_rows[:, :, c]) \
                  .then_inc(keys_staged, 1)
                ga.tensor_copy(dkey_now[:], dkey[:, 0:2] if isinstance(i, int) else dkey[:, d]) \
                  .then_inc(keys_staged, 1)
                pool.wait_ge(keys_staged, 2 * i + 2)
                if not isinstance(i, int):
                    settle(1)

            def table_rows(b):
                ga.tensor_scalar(oh[:, b, :, :], key_now[:, :, b * P:(b + 1) * P], pcol[:, 0:1], None,
                                 ALU.is_equal).then_inc(oh_made, 1)

            def targets(b):
                ga.tensor_scalar(sc_l[:, b, :], irow[:, 1:P + 1], dkey_now[:, b:b + 1], None,
                                 ALU.is_equal).then_inc(dl_made, 1)

            def settle(n):
                ga.tensor_tensor(spare[0:1, n:n + 1], zero_r[0:1, 0:1], zero_r[0:1, 1:2], ALU.add)

            pool.wait_ge(keys_back, 16)
            stage_keys(0)
            for b in range(2):
                table_rows(b)
                targets(b)
            with pool.Fori(1, NT // 2) as i:
                pool.wait_ge(oh_made, 2 * i)
                pool.wait_ge(dl_made, 2 * i)
                settle(0)
                stage_keys(i)
                for b in range(2):
                    pool.wait_ge(gathered, JO + 2 * i - 1 + b)
                    settle(2 + b)
                    table_rows(b)
                    pool.wait_ge(scattered, 1 + JO + 2 * i - 1 + b)
                    settle(4 + b)
                    targets(b)

        @block.scalar
        def _(act):
            sa = nc.scalar
            for k, v in enumerate((src, dst)):
                act.dma_start(edges[:, k, :], v[E_ST:E].rearrange("(p j) -> p j", p=P)).then_inc(edges_in, 16)
            for k, v in enumerate((src, dst)):
                act.dma_start(st_row[:, k, :], v[0:E_ST].partition_broadcast(P)).then_inc(st_rows_in, 16)
                act.dma_start(st_col[:, k, 0:1], v[0:E_HH].rearrange("(p j) -> p j", p=P)).then_inc(consts_in, 16)
                act.dma_start(st_col[:, k, 1:], v[E_HH:E_ST].rearrange("(p j) -> p j", p=P)).then_inc(consts_in, 16)
            act.dma_start(wa_bc[:], W_a.rearrange("d o -> (d o)").partition_broadcast(P)).then_inc(consts_in, 16)
            act.dma_start(ba_bc[:], b_a.partition_broadcast(P)).then_inc(consts_in, 16)
            for k, v in enumerate((b_hn, b_on)):
                with nc.allow_non_contiguous_dma("1024 bias values, once"):
                    act.dma_start(bnT[:, k, :], v.rearrange("(c p) -> p c", p=P)).then_inc(consts_in, 16)
            act.dma_start(bias_bc[:, 0, :], b_ho.partition_broadcast(P)).then_inc(biases_in, 16)
            act.dma_start(bias_bc[:, 1, :], b_oo.partition_broadcast(P)).then_inc(biases_in, 16)

            act.wait_ge(pe_step, pe_at("xT"))
            sa.copy(x_T[:].rearrange("p c n -> p (c n)"), G0).then_inc(act_step, 1)

            def table_high(tab, acc, when, eng_sem):
                act.wait_ge(eng_sem, when)
                for q in range(4):
                    r = (q % 2) * Q
                    ins = sa.copy(tab[0:Q, q, :], acc[r:r + Q, (q // 2) * D:(q // 2 + 1) * D])
                ins.then_inc(act_step, 1)

            table_high(A_tab, G0, PAIRS["hoA"], w_used)
            act.wait_ge(dve_step, dve_at("key_u8"))
            act.dma_start(key_dram.rearrange("k t m -> t k m"), key_u8[:]).then_inc(keys_out, 16)
            act.wait_ge(keys_out, 16)
            act.dma_start(key_rows[:].rearrange("p k n -> p (k n)"),
                          key_dram.rearrange("k t m -> (k t m)").partition_broadcast(P)).then_inc(keys_back, 16)
            table_high(B_tab, G1, dve_at("hoB_b"), dve_step)
            act.dma_start(bias_bc[:, 0, :], b_hh.partition_broadcast(P)).then_inc(biases_in, 16)
            act.wait_ge(pe_step, pe_at("ghT"))
            act.wait_ge(dve_step, dve_at("steer"))
            sa.copy(hh_T[:].rearrange("p a c n -> p (a c n)"), G0).then_inc(act_step, 1)
            act.wait_ge(w_used, PAIRS["ooA"])
            sa.copy(Ao_tab[:, :, 0, :], G0.rearrange("p (h d) -> p h d", h=2)).then_inc(act_step, 1)
            act.wait_ge(dve_step, dve_at("ooB_b"))
            sa.copy(Bo_tab[:, :, 0, :], G1.rearrange("p (h d) -> p h d", h=2)).then_inc(act_step, 1)

            act.wait_ge(dve_step, dve_at("masked"))
            for h in range(2):
                ins = sa.activation(S_log[:, :, h, :], S_log[:, :, h, :], ACT.Exp, bias=small[:, h:h + 1])
            ins.then_inc(act_step, 1)
            act.wait_ge(pe_step, pe_at("zT"))
            sa.copy(z_T[:].rearrange("p c n -> p (c n)"), G1).then_inc(act_step, 1)
            act.wait_ge(w_used, PAIRS["upd"])
            for c in range(KC):
                for k, (a, b) in enumerate(((0, NH), (NH, N))):
                    ins = sa.activation(o_T[:, c, a:b], G0[:, c * N + a:c * N + b], ACT.Relu, bias=bnT[:, k, c:c + 1])
            ins.then_inc(act_step, 1)
            act.wait_ge(dve_step, dve_at("var0"))
            sa.activation(small[:, 8:10], small[:, 4:6], ACT.Sqrt, bias=eps_ln[:, 0:1]).then_inc(act_step, 1)
            act.wait_ge(pe_step, pe_at("x1T"))
            sa.copy(x_T[:].rearrange("p c n -> p (c n)"), G0).then_inc(act_step, 1)
            act.wait_ge(w_used, PAIRS["h1"])
            sa.copy(h1[:].rearrange("p h d -> p (h d)"), G1).then_inc(act_step, 1)
            act.wait_ge(dve_step, dve_at("lr"))
            sa.activation(PT[:], PT[:], ACT.Exp, scale=-1.0).then_inc(act_step, 1)
            act.wait_ge(dve_step, dve_at("hpn"))
            sa.activation(y2[:], y2[:], ACT.Exp).then_inc(act_step, 1)
            act.wait_ge(dve_step, dve_at("var1"))
            sa.activation(small[:, 8:10], small[:, 4:6], ACT.Sqrt, bias=eps_ln[:, 0:1]).then_inc(act_step, 1)

        @block.vector
        def _(dve):
            v = nc.vector
            mine = [0]

            def link(ins):
                mine[0] += 1
                ins.then_inc(dve_done, 1)
                dve.wait_ge(dve_done, mine[0])

            def stage():
                v.nop().then_inc(dve_step, 1)

            dve.wait_ge(edges_in, 32)
            link(v.tensor_scalar(eq_i[:], edges[:], 6, None, ALU.logical_shift_right))
            link(v.tensor_scalar(el_i[:], edges[:], Q - 1, None, ALU.bitwise_and))
            link(v.scalar_tensor_tensor(cls[:], eq_i[:, 0, :], 4.0, eq_i[:, 1, :], ALU.mult, ALU.add))
            link(v.tensor_scalar(val[:], el_i[:], 1.0, None, ALU.add))
            dve.wait_ge(setup_done, 1)
            link(v.tensor_tensor(cls_oh[:], cls[:].unsqueeze(1).broadcast_to([P, NC, JH]),
                                 irow[:, 0:NC].unsqueeze(2).broadcast_to([P, NC, JH]), ALU.is_equal))
            link(v.tensor_tensor_scan(cum[:].rearrange("p c j -> p (c j)"), gate[:].rearrange("p c j -> p (c j)"),
                                      cls_oh[:].rearrange("p c j -> p (c j)"), 0.0, ALU.mult, ALU.add))
            link(v.tensor_copy(tot[:], cum[:, :, JH - 1]))
            stage()
            dve.wait_ge(pe_step, pe_at("totals"))
            pre, allc = ps[:, 3584:3584 + NC], ps[:, 3584 + NC:3584 + 2 * NC]
            link(v.tensor_scalar(cwi[:, 0, :], allc, float(P - 1), None, ALU.add))
            link(v.tensor_scalar(cwi[:, 1, :], cwi[:, 0, :], 7, None, ALU.logical_shift_right))
            link(v.tensor_copy(cw[:, 0, :], cwi[:, 1, :]))
            link(v.memset(cw[:, 5, :], 1.0))
            link(v.tensor_tensor_scan(cw[:, 1, :], cw[:, 5, :], cw[:, 0, :], 0.0, ALU.mult, ALU.add))
            link(v.tensor_tensor(cw[:, 2, :], cw[:, 1, :], cw[:, 0, :], ALU.subtract))
            link(v.tensor_scalar(cw[:, 3, :], cw[:, 2, :], float(P), -1.0, ALU.mult, ALU.add))
            link(v.tensor_tensor(cw[:, 4, :], cw[:, 3, :], pre, ALU.add))
            link(v.tensor_tensor(cum[:], cum[:], cw[:, 4, :].unsqueeze(2).broadcast_to([P, NC, JH]), ALU.add))
            link(v.tensor_tensor(cum[:], cum[:], cls_oh[:], ALU.mult))
            link(v.tensor_reduce(slot[:], cum[:].rearrange("p c j -> p j c"), AX, ALU.add))
            link(v.tensor_copy(slot_i[:, 0, :], slot[:]))
            link(v.tensor_scalar(slot_i[:, 1, :], slot_i[:, 0, :], 7, None, ALU.logical_shift_right))
            link(v.tensor_scalar(slot_i[:, 2, :], slot_i[:, 0, :], P - 1, None, ALU.bitwise_and))
            link(v.tensor_copy(slot_f[:], slot_i[:, 1:3, :]))
            link(v.tensor_tensor(pos_oh[:], slot_f[:, 1, :].unsqueeze(2).broadcast_to([P, JH, P]),
                                 irow[:, 0:P].unsqueeze(1).broadcast_to([P, JH, P]), ALU.is_equal))
            for k in range(2):
                link(v.tensor_tensor(tile_val[:, :, k, :], slot_f[:, 0, :].unsqueeze(2).broadcast_to([P, JH, NT]),
                                     irow[:, 0:NT].unsqueeze(1).broadcast_to([P, JH, NT]), ALU.is_equal))
                link(v.tensor_tensor(tile_val[:, :, k, :], tile_val[:, :, k, :],
                                     val[:, k, :].unsqueeze(2).broadcast_to([P, JH, NT]), ALU.mult))
            stage()
            link(v.tensor_tensor(cle[:], cw[:, 1, :].unsqueeze(1).broadcast_to([P, NT, NC]),
                                 irow[:, 0:NT].unsqueeze(2).broadcast_to([P, NT, NC]), ALU.is_le))
            link(v.tensor_reduce(tcls[:, 0, :], cle[:], AX, ALU.add))
            link(v.tensor_scalar(tcls_i[:, 0, :], tcls[:, 0, :], float(NC - 1), None, ALU.min))
            link(v.tensor_scalar(tcls_i[:, 1, :], tcls_i[:, 0, :], 2, None, ALU.logical_shift_right))
            link(v.tensor_scalar(tcls_i[:, 2, :], tcls_i[:, 0, :], 3, None, ALU.bitwise_and))
            link(v.tensor_scalar(tcls_i[:, 3, :], tcls_i[:, 2, :], 1, None, ALU.bitwise_and))
            link(v.tensor_scalar(tcls_i[:, 4, :], tcls_i[:, 2, :], 1, None, ALU.logical_shift_right))
            link(v.scalar_tensor_tensor(tcls_i[:, 0, :], tcls_i[:, 4, :], 4.0, tcls_i[:, 1, :], ALU.mult, ALU.add))
            link(v.memset(steer[:], 0))
            tv = tcls_i[0:1, :, :].rearrange("p c (i b) -> p c i b", b=2)
            for b in range(2):
                link(v.tensor_copy(steer[0:1, 0:NT // 2, b], tv[:, 1, :, b]))
                link(v.tensor_copy(steer[0:1, 0:NT // 2, 2 + b], tv[:, 2, :, b]))
                link(v.tensor_copy(steer[0:1, 1:NT // 2 + 1, 4 + b], tv[:, 0, :, b]))
            link(v.tensor_scalar(tcls[:, 1, :], tcls_i[:, 3, :], float(Q), None, ALU.mult))
            dve.wait_ge(pe_step, pe_at("perm"))
            link(v.tensor_copy(key_col[:].rearrange("p k t -> p (k t)"), ps[:, 3072:3072 + 2 * NT]))
            stage()
            link(v.tensor_tensor(dkey[:], key_col[:, 1, :], tcls[:, 1, :], ALU.add))
            dve.wait_ge(pe_step, pe_at("keysT"))
            link(v.tensor_copy(key_u8[:].rearrange("t k m -> t (k m)"), ps[0:NT, 3584:3584 + 2 * P]))
            stage()
            dve.wait_ge(consts_in, 128)
            link(v.tensor_copy(st_colf[:], st_col[:]))
            dve.wait_ge(keys_out, 16)
            stage()

            def table_low(tab, acc, act_stage):
                dve.wait_ge(act_step, act_at(act_stage))
                for q in range(4):
                    r = (q % 2) * Q
                    link(v.tensor_tensor(tab[Q:P, q, :], acc[r:r + Q, (q // 2) * D:(q // 2 + 1) * D],
                                         tab[0:Q, q, :].bitcast(F32), ALU.subtract))
                stage()

            def add_bias(acc, k):
                for h in range(2):
                    link(v.tensor_tensor(acc[:, h * D:(h + 1) * D], acc[:, h * D:(h + 1) * D], bias_bc[:, k, :],
                                         ALU.add))
                stage()

            def table_low_nat(tab, acc, act_stage):
                dve.wait_ge(act_step, act_at(act_stage))
                for h in range(2):
                    link(v.tensor_tensor(tab[:, h, 1, :], acc[:, h * D:(h + 1) * D],
                                         tab[:, h, 0, :].bitcast(F32), ALU.subtract))
                stage()

            table_low(A_tab, G0, "hoA_hi")
            dve.wait_ge(w_used, PAIRS["hoB"])
            dve.wait_ge(biases_in, 32)
            add_bias(G1, 0)
            table_low(B_tab, G1, "hoB_hi")
            table_low_nat(Ao_tab, G0, "ooA_hi")
            dve.wait_ge(w_used, PAIRS["ooB"])
            add_bias(G1, 1)
            table_low_nat(Bo_tab, G1, "ooB_hi")
            dve.wait_ge(biases_in, 48)

            for t in range(1 + JO):
                acc = ps[:, (t % 2) * D:(t % 2 + 1) * D]
                if t == 0:
                    dve.wait_ge(w_used, PAIRS["hh"])
                    link(v.tensor_tensor(acc, acc, bias_bc[:, 0, :], ALU.add))
                else:
                    dve.wait_ge(gathered, t)
                link(v.scalar_tensor_tensor(junk[:], acc, 0.0, wa_bc[:], ALU.max, ALU.mult,
                                            accum_out=st_logit[:, t:t + 1]))
                v.nop().then_inc(reduced, 1)
                if t >= 1:
                    dve.wait_ge(scattered, t)
                v.tensor_scalar(st_scl[:], irow[:, 0:N], st_colf[:, 1, t:t + 1], None, ALU.is_equal) \
                 .then_inc(sc_made, 1)
                v.tensor_scalar(st_scr[:, 0, :], irow[:, 0:N], st_colf[:, 0, t:t + 1], st_logit[:, t:t + 1],
                                ALU.is_equal, ALU.mult).then_inc(sc_made, 1)
                v.tensor_scalar(st_scr[:, 1, :], irow[:, 0:N], st_colf[:, 0, t:t + 1], None,
                                ALU.is_equal).then_inc(sc_made, 1)
            dve.wait_ge(scattered, 1)
            v.tensor_copy(S_log[:, 0, :, :].rearrange("p h n -> p (h n)"), G1[:, 1024:1536])
            link(v.tensor_copy(S_cnt[:, 0, :, :].rearrange("p h n -> p (h n)"), G1[:, 1536:2048]))
            stage()
            dve.wait_ge(scattered, 1 + JO)
            v.tensor_copy(S_log[:, 1, :, :].rearrange("p h n -> p (h n)"), G1[:, 0:512])
            link(v.tensor_copy(S_cnt[:, 1, :, :].rearrange("p h n -> p (h n)"), G1[:, 512:1024]))
            stage()

            def edge_tile(t, b, first):
                acc = ps[:, b * D:(b + 1) * D]
                dve.wait_ge(gathered, JO + 1 + t)
                v.scalar_tensor_tensor(junk[:], acc, 0.0, wa_bc[:], ALU.max, ALU.mult,
                                       accum_out=logit[:, bass.ds(t, 1)]).then_inc(reduced, 1)
                dve.wait_ge(reduced, 1 + JO + 1 + t)
                if not first:
                    dve.wait_ge(scattered, 1 + JO + t - 1)
                v.tensor_scalar(sc_r[:, b, 0, :], irow[:, 1:Q + 1], key_col[:, 0, bass.ds(t, 1)],
                                logit[:, bass.ds(t, 1)], ALU.is_equal, ALU.mult).then_inc(sc_made, 1)
                v.tensor_scalar(sc_r[:, b, 1, :], irow[:, 1:Q + 1], key_col[:, 0, bass.ds(t, 1)], None,
                                ALU.is_equal).then_inc(sc_made, 1)

            for b in range(2):
                edge_tile(b, b, True)
            with dve.Fori(1, NT // 2) as i:
                for b in range(2):
                    edge_tile(2 * i + b, b, False)
            dve.wait_ge(scattered, 1 + JO + NT)
            v.tensor_copy(S_log[:, 2, :, :].rearrange("p h n -> p (h n)"), G1[:, 0:512])
            link(v.tensor_copy(S_cnt[:, 2, :, :].rearrange("p h n -> p (h n)"), G1[:, 512:1024]))
            stage()

            Lf, Cf = S_log[:].rearrange("p k h n -> p (k h n)"), S_cnt[:].rearrange("p k h n -> p (k h n)")
            scratch = y1[:].rearrange("p h d -> p (h d)")[:, 0:3 * 2 * N]
            link(v.tensor_scalar(scratch, Cf, 1.0, None, ALU.max))
            link(v.reciprocal(scratch, scratch))
            link(v.tensor_tensor(Lf, Lf, scratch, ALU.mult))
            link(v.tensor_scalar(Lf, Lf, ba_bc[:, 0:1], None, ALU.add))
            link(v.tensor_scalar(scratch, Cf, 0.0, -BIG, ALU.is_equal, ALU.mult))
            link(v.tensor_tensor(Lf, Lf, scratch, ALU.add))
            for h in range(2):
                link(v.tensor_reduce(small[:, 2 + h:3 + h], S_log[:, :, h, :], mybir.AxisListType.XY, ALU.max))
            link(v.tensor_scalar(small[:, 0:2], small[:, 2:4], -1.0, None, ALU.mult))
            stage()
            dve.wait_ge(act_step, act_at("soft"))
            link(v.tensor_tensor(Lf, Lf, Cf, ALU.mult))
            link(v.tensor_tensor(S_log[:, 0, :, :], S_log[:, 0, :, :], S_log[:, 1, :, :], ALU.add))
            link(v.tensor_tensor(S_log[:, 0, :, :], S_log[:, 0, :, :], S_log[:, 2, :, :], ALU.add))
            link(v.tensor_reduce(small[:, 4:6], S_log[:, 0, :, :], AX, ALU.add))
            link(v.tensor_scalar(small[:, 6:8], small[:, 4:6], 0.0, None, ALU.is_equal))
            link(v.tensor_tensor(small[:, 4:6], small[:, 4:6], small[:, 6:8], ALU.add))
            link(v.reciprocal(small[:, 6:8], small[:, 4:6]))
            for h in range(2):
                link(v.tensor_scalar(S_log[:, 0, h, :], S_log[:, 0, h, :], small[:, 6 + h:7 + h], None, ALU.mult))
            stage()
            link(v.tensor_tensor(S_cnt[:, 0, :, :], S_cnt[:, 0, :, :], S_cnt[:, 1, :, :], ALU.add))
            link(v.tensor_tensor(S_cnt[:, 0, :, :], S_cnt[:, 0, :, :], S_cnt[:, 2, :, :], ALU.add))
            dve.wait_ge(pe_step, pe_at("PT"))
            link(v.tensor_copy(PT[:].rearrange("p h n -> p (h n)"), G0[:, 0:512]))
            stage()

            def norm(res, dest):
                for h in range(2):
                    for g in range(2):
                        link(v.bn_stats(small[:, 16 + 12 * h + 6 * g:22 + 12 * h + 6 * g],
                                        res[:, h, g * 512:(g + 1) * 512]))
                    link(v.bn_aggr(small[:, 40 + 2 * h:42 + 2 * h], small[:, 16 + 12 * h:28 + 12 * h]))
                    link(v.tensor_copy(small[:, 4 + h:5 + h], small[:, 41 + 2 * h:42 + 2 * h]))
                stage()
                dve.wait_ge(act_step, act_at(dest[1]))
                link(v.reciprocal(small[:, 10:12], small[:, 8:10]))
                for h in range(2):
                    link(v.tensor_scalar(dest[0][:, h, :], res[:, h, :], small[:, 40 + 2 * h:41 + 2 * h],
                                         small[:, 10 + h:11 + h], ALU.subtract, ALU.mult))

            dve.wait_ge(pe_step, pe_at("nat"))
            link(v.tensor_tensor(y1[:].rearrange("p h d -> p (h d)"), G1, x_nat[:].rearrange("p h d -> p (h d)"),
                                 ALU.add))
            stage()
            norm(y1, (x1, "sd0"))
            stage()

            dve.wait_ge(act_step, act_at("h1"))
            dve.wait_ge(biases_in, 80)
            for k in range(2):
                for h in range(2):
                    link(v.scalar_tensor_tensor(y1[:, h, :], h1[:, h, :], 1.0, bias_bc[:, k, :], ALU.mult, ALU.mult,
                                                accum_out=small[:, 12 + 2 * k + h:13 + 2 * k + h]))
            for h in range(2):
                link(v.tensor_scalar(y2[:, 0, h * P:(h + 1) * P], ident[:], small[:, 12 + h:13 + h], None, ALU.mult))
            stage()
            dve.wait_ge(pe_step, pe_at("albc"))
            for h in range(2):
                link(v.tensor_scalar(PT[:, h, :], G0[:, 0:N], small[:, 14 + h:15 + h], None, ALU.add))
            link(v.scalar_tensor_tensor(PT[:], PT[:], SLOPE, PT[:], ALU.mult, ALU.max))
            stage()
            dve.wait_ge(act_step, act_at("lrelu"))
            link(v.tensor_tensor(PT[:], PT[:], S_cnt[:, 0, :, :], ALU.mult))
            stage()
            dve.wait_ge(pe_step, pe_at("hp"))
            link(v.tensor_scalar(small[:, 4:6], G0[:, 512:1024].rearrange("p (h n) -> p h n", h=2)[:, :, 0],
                                 EPS_L1, None, ALU.add))
            link(v.reciprocal(small[:, 6:8], small[:, 4:6]))
            for h in range(2):
                link(v.tensor_scalar(y1[:, h, :], G1[:, h * D:(h + 1) * D], small[:, 6 + h:7 + h], None, ALU.mult))
            link(v.tensor_scalar(y2[:], y1[:], 0.0, None, ALU.min))
            stage()
            link(v.scalar_tensor_tensor(x1[:], y1[:], 0.0, x1[:], ALU.max, ALU.add))
            dve.wait_ge(act_step, act_at("elu"))
            link(v.scalar_tensor_tensor(y1[:], y2[:], -1.0, x1[:], ALU.add, ALU.add))
            stage()
            norm(y1, (y2, "sd1"))
            stage()

        @block.tensor
        def _(pe):
            mm = nc.tensor.matmul
            used = [0]

            def pair_used(ins, name, k):
                if k % 2:
                    assert turn[name, k - 1] == used[0], (name, k)
                    used[0] += 1
                    ins.then_inc(w_used, 1)

            def stage(ins):
                ins.then_inc(pe_step, 1)

            pe.wait_ge(x_in, 16)
            pe.wait_ge(setup_done, 1)
            for c in range(KC):
                for h in range(2):
                    ins = nc.tensor.transpose(G0[:, c * N + h * P:c * N + (h + 1) * P], x_nat[:, h, c * P:(c + 1) * P],
                                              ident[:])
            stage(ins)
            pe.wait_ge(dve_step, dve_at("tot"))
            mm(ps[:, 3584:3584 + NC], tri[:], tot[:], start=True, stop=True)
            stage(mm(ps[:, 3584 + NC:3584 + 2 * NC], ones_b[:], tot[:], start=True, stop=True))
            pe.wait_ge(act_step, act_at("xT"))

            def dense(name, k0, acc):
                for c in range(KC):
                    w_arrived(pe, name, k0 + c)
                    for h in range(2):
                        for n in range(2):
                            ins = mm(acc[:, h * D + n * 512:h * D + (n + 1) * 512], x_T[:, c, h * P:(h + 1) * P],
                                     chunk(name, k0 + c)[:, n * 512:(n + 1) * 512], start=(c == 0), stop=(c == KC - 1))
                    pair_used(ins, name, k0 + c)
                return ins

            dense("ho", 0, G0)
            pe.wait_ge(dve_step, dve_at("perm_in"))
            for j in range(JH):
                ins = mm(ps[:, 3072:3072 + 2 * NT], pos_oh[:, j, :], tile_val[:, j, :, :].rearrange("p k t -> p (k t)"),
                         start=(j == 0), stop=(j == JH - 1))
            stage(ins)
            pe.wait_ge(dve_step, dve_at("key_col"))
            for k in range(2):
                ins = nc.tensor.transpose(ps[0:NT, 3584 + k * P:3584 + (k + 1) * P], key_col[:, k, :], ident[:])
            stage(ins)
            pe.wait_ge(dve_step, dve_at("key_u8"))
            dense("ho", KC, G1)
            pe.wait_ge(st_oh, 4)
            pe.wait_ge(dve_step, dve_at("hoA_lo"))
            for k in range(2):
                for c in range(KC):
                    for h in range(2):
                        ins = mm(G0[:, (k * KC + c) * P:(k * KC + c + 1) * P], x_nat[:, h, c * P:(c + 1) * P],
                                 st_ohT[:, k, h, :], start=(h == 0), stop=(h == 1))
            stage(ins)
            pe.wait_ge(act_step, act_at("ghT"))
            dense("oo", 0, G0)
            pe.wait_ge(dve_step, dve_at("hoB_lo"))
            dense("oo", KC, G1)
            pe.wait_ge(dve_step, dve_at("ooA_lo"))
            for k in range(2 * KC):
                w_arrived(pe, "hh", k)
                for n in range(2):
                    ins = mm(ps[:, n * 512:(n + 1) * 512], hh_T[:, k // KC, k % KC, :],
                             chunk("hh", k)[:, n * 512:(n + 1) * 512], start=(k == 0), stop=(k == 2 * KC - 1))
                pair_used(ins, "hh", k)
            pe.wait_ge(dve_step, dve_at("ooB_lo"))

            def scatter_static(t):
                base = 1024 if t == 0 else 0
                pe.wait_ge(sc_made, 3 * (t + 1))
                for r in range(2):
                    for h in range(2):
                        ins = mm(G1[:, base + r * 512 + h * N:base + r * 512 + (h + 1) * N],
                                 st_scl[:, h * P:(h + 1) * P], st_scr[:, r, :],
                                 start=(t <= 1 and h == 0), stop=(t == 0 or t == JO), skip_group_check=True)
                ins.then_inc(scattered, 1)

            for t in range(1, JO + 1):
                acc = ps[:, (t % 2) * D:(t % 2 + 1) * D]
                pe.wait_ge(st_oh, 4 + 4 * t)
                if t >= 2:
                    pe.wait_ge(reduced, t - 1)
                for i, (k, h, part) in enumerate((k, h, part) for k in range(2) for h in range(2) for part in range(2)):
                    tab = (Ao_tab, Bo_tab)[k]
                    for n in range(2):
                        ins = mm(acc[:, n * 512:(n + 1) * 512], st_ohTr[:, k, h, :],
                                 tab[:, h, part, n * 512:(n + 1) * 512], start=(i == 0), stop=(i == 7))
                ins.then_inc(gathered, 1)
                scatter_static(t - 1)
            scatter_static(JO)
            pe.wait_ge(dve_step, dve_at("D_oo"))

            for r in range(2):
                mm(G1[:, r * 512:(r + 1) * 512], zero_r[0:1, 0:P], zero_r[0:1, :], start=True, stop=False,
                   skip_group_check=True)
            pe.wait_ge(act_step, act_at("hoB_hi"))

            def gather(t, b, sq, dq, first):
                pe.wait_ge(oh_made, t + 1)
                if first:
                    pe.wait_ge(reduced, JO + b)
                else:
                    pe.wait_ge(reduced, 1 + JO + t - 1)
                for k, (tab, q) in enumerate(((A_tab, sq), (B_tab, dq))):
                    for n in range(2):
                        ins = mm(ps[:, b * D + n * 512:b * D + (n + 1) * 512], oh[:, b, k, :],
                                 tab[:].rearrange("p q d -> p (q d)")[:, bass.ds(q * D + n * 512, 512)],
                                 start=(tab is A_tab), stop=(tab is B_tab))
                ins.then_inc(gathered, 1)

            def scatter(t, b, block64):
                pe.wait_ge(dl_made, t + 1)
                pe.wait_ge(sc_made, 3 * (1 + JO) + 2 * (t + 1))
                for r in range(2):
                    ins = mm(G1[:, bass.ds(r * 512 + block64 * Q, Q)], sc_l[:, b, :], sc_r[:, b, r, :],
                             start=False, stop=False, skip_group_check=True)
                ins.then_inc(scattered, 1)

            def steered(i, lo, hi):
                return [pe.value_load(steer[0:1, i, c:c + 1] if isinstance(i, int)
                                      else steer[0:1, bass.ds(i, 1), c:c + 1], min_val=0, max_val=m)
                        for c, m in ((0, 3), (1, 3), (2, 3), (3, 3), (4, 7), (5, 7))[lo:hi]]

            s0, s1, d0, d1 = steered(0, 0, 4)
            gather(0, 0, s0, d0, True)
            gather(1, 1, s1, d1, True)
            with pe.Fori(1, NT // 2) as i:
                s0, s1, d0, d1, o0, o1 = steered(i, 0, 6)
                gather(2 * i, 0, s0, d0, False)
                scatter(2 * i - 2, 0, o0)
                gather(2 * i + 1, 1, s1, d1, False)
                scatter(2 * i - 1, 1, o1)
            o0, o1 = steered(NT // 2, 4, 6)
            scatter(NT - 2, 0, o0)
            scatter(NT - 1, 1, o1)

            pe.wait_ge(dve_step, dve_at("P"))
            for hs in range(2):
                for hd in range(2):
                    ins = nc.tensor.transpose(G0[:, hs * N + hd * P:hs * N + (hd + 1) * P],
                                              S_log[:, 0, hd, hs * P:(hs + 1) * P], ident[:])
            stage(ins)
            pe.wait_ge(dve_step, dve_at("PT"))
            for c in range(KC):
                for hs in range(2):
                    ins = mm(G1[:, c * N:(c + 1) * N], x_nat[:, hs, c * P:(c + 1) * P], PT[:, hs, :],
                             start=(hs == 0), stop=(hs == 1))
            stage(ins)
            for n in range(4):
                mm(G0[:, n * 512:(n + 1) * 512], zero_r[0:1, 0:P], zero_r[0:1, :], start=True, stop=False,
                   skip_group_check=True)
            for k in range(0, 2 * KC, 2):
                rhs = x_T if k < KC else z_T
                if k == KC:
                    pe.wait_ge(act_step, act_at("zT"))
                for name, a, b in (("hn", 0, NH), ("on", NH, N)):
                    w_arrived(pe, name, k)
                    for kk in (k, k + 1):
                        for c in range(KC):
                            ins = mm(G0[:, c * N + a:c * N + b], chunk(name, kk)[:, c * P:(c + 1) * P],
                                     rhs[:, kk % KC, a:b], start=False, stop=(kk == 2 * KC - 1), skip_group_check=True)
                    pair_used(ins, name, k + 1)
            pe.wait_ge(act_step, act_at("upd"))
            for h in range(2):
                for c in range(KC):
                    ins = nc.tensor.transpose(G1[:, h * D + c * P:h * D + (c + 1) * P], o_T[:, c, h * P:(h + 1) * P],
                                              ident[:])
            stage(ins)
            pe.wait_ge(dve_step, dve_at("x1"))
            for c in range(KC):
                for h in range(2):
                    ins = nc.tensor.transpose(G0[:, c * N + h * P:c * N + (h + 1) * P], x1[:, h, c * P:(c + 1) * P],
                                              ident[:])
            stage(ins)
            pe.wait_ge(act_step, act_at("x1T"))
            dense("l1", 0, G1)
            pe.wait_ge(dve_step, dve_at("al"))
            stage(mm(G0[:, 0:N], ones_f[:], y2[:, 0, 0:N], start=True, stop=True))
            pe.wait_ge(dve_step, dve_at("ET"))
            for hs in range(2):
                for hd in range(2):
                    mm(G0[:, 512 + hs * N:512 + hs * N + 1], PT[:, hd, hs * P:(hs + 1) * P], ones_f[:, 0:1],
                       start=(hd == 0), stop=(hd == 1))
            for hs in range(2):
                for n in range(2):
                    for hd in range(2):
                        ins = mm(G1[:, hs * D + n * 512:hs * D + (n + 1) * 512], PT[:, hd, hs * P:(hs + 1) * P],
                                 h1[:, hd, n * 512:(n + 1) * 512], start=(hd == 0), stop=(hd == 1))
            stage(ins)


_INS = ['x', 'src', 'dst', 'L0_gnn_W_hh', 'L0_gnn_b_hh', 'L0_gnn_W_oo', 'L0_gnn_b_oo', 'L0_gnn_W_ho', 'L0_gnn_b_ho',
        'L0_gnn_W_a', 'L0_gnn_b_a', 'L0_gnn_W_hn', 'L0_gnn_b_hn', 'L0_gnn_W_on', 'L0_gnn_b_on', 'L1_gnn_W', 'L1_gnn_a']


def kernel(**inputs):
    import numpy as _np
    import concourse.bacc as _bacc
    from concourse import mybir as _mybir
    from concourse.bass_utils import run_bass_kernel_spmd as _run

    nc = _bacc.Bacc("TRN2", target_bir_lowering=False, num_devices=1)
    arrays, args = {}, []
    for name in _INS:
        a = _np.ascontiguousarray(inputs[name])
        arrays[f"in_{name}_dram"] = a
        args.append(nc.dram_tensor(f"in_{name}_dram", a.shape, _mybir.dt.from_np(a.dtype), kind="ExternalInput").ap())
    args.append(nc.dram_tensor("out_0_dram", (N, D), F32, kind="ExternalOutput").ap())
    gnn_two_layers(nc, *args)
    r = _run(nc, [arrays], core_ids=[0])
    return r.results[0]["out_0_dram"]
```

```python
from contextlib import ExitStack

import concourse.bass as bass
from concourse import mybir

P = 128
N = 256
D = 1024
E = 8192
NH = 64
E_HH, E_OO = 128, 640
E_ST = E_HH + E_OO
E_HO = E - E_ST
JH = E_HO // P
JS = JH // 2
JO = E_OO // P
Q = 64
NC = (N // Q) ** 2
U = 4
NT = -(-(JH + NC - 1) // U) * U
TURNS = NT // U
KC = D // P
NS = 4
NB = 4
SLOPE, EPS_L1, EPS_LN = 0.1, 1e-5, 1e-5
BIG = 3.0e38

F32 = mybir.dt.float32
F32R = mybir.dt.float32r
BF16 = mybir.dt.bfloat16
I32 = mybir.dt.int32
U8 = mybir.dt.uint8
ALU = mybir.AluOpType
ACT = mybir.ActivationFunctionType
AX = mybir.AxisListType.X
AXY = mybir.AxisListType.XY


def gnn_two_layers(nc, x, src, dst, W_hh, b_hh, W_oo, b_oo, W_ho, b_ho, W_a, b_a, W_hn, b_hn, W_on, b_on,
                   L1_W, L1_a, out):
    ctx = ExitStack()
    with ctx:
        def sb(name, shape, dt=F32, stack=ctx):
            return stack.enter_context(nc.sbuf_tensor(name, shape, dt))

        def sem(name):
            return ctx.enter_context(nc.semaphore(name))

        x_nat = sb("x_nat", [P, 2, D])
        xT_hi = sb("xT_hi", [P, KC, N], F32R)
        xT_lo = sb("xT_lo", [P, KC, N], F32R)
        W_raw = sb("W_raw", [P, NS, 2, D])
        W_hi = sb("W_hi", [P, NB, D], F32R)
        W_lo = sb("W_lo", [P, NB, D], F32R)
        wa_bc = sb("wa_bc", [P, D])
        bias_bc = sb("bias_bc", [P, 2, D])
        ident = sb("ident", [P, P])
        irow = sb("irow", [P, N + 1])
        pcol = sb("pcol", [P, 4])
        tri = sb("tri", [P, P], BF16)
        ones_b = sb("ones_b", [P, P], BF16)
        ones_f = sb("ones_f", [P, P])
        zero_b = sb("zero_b", [1, 512], BF16)
        spare = sb("spare", [1, 16])
        st_col = sb("st_col", [P, 2, 1 + JO], I32)
        st_colf = sb("st_colf", [P, 2, 1 + JO])
        keys = sb("keys", [P, NT, 2])
        keys_now = sb("keys_now", [P, U, 2])
        steer = sb("steer", [1, TURNS + 1, 3, U], I32)
        logit_now = sb("logit_now", [P, U])
        st_logit = sb("st_logit", [P, 1 + JO])
        part_f = sb("part_f", [P, 2])
        part_b = sb("part_b", [P, 2], BF16)
        oh_dist = sb("oh_dist", [P, 2, 2, P], BF16)
        oh = sb("oh", [P, 2, 2, P], F32R)
        sc_l = sb("sc_l", [P, U, P])
        sc_r = sb("sc_r", [P, U, 2, Q])
        junk = sb("junk", [P, 2, D], BF16)
        small = sb("small", [P, 64])
        eps_ln = sb("eps_ln", [P, 1])
        ba_bc = sb("ba_bc", [P, 1])
        S_log = sb("S_log", [P, 3, 2, N])
        S_cnt = sb("S_cnt", [P, 3, 2, N])
        top = sb("top", [P, 2, 2])

        regions = ExitStack()
        A_tab = sb("A_tab", [P, 4, D], F32R, regions)
        B_tab = sb("B_tab", [P, 4, D], F32R, regions)
        Ao_tab = A_tab[:].rearrange("p (h k) d -> p h k d", h=2)
        Bo_tab = B_tab[:].rearrange("p (h k) d -> p h k d", h=2)
        hh_hi = B_tab[:, 0:2, :].rearrange("p a (c n) -> p a c n", c=KC)
        hh_lo = B_tab[:, 2:4, :].rearrange("p a (c n) -> p a c n", c=KC)
        st_row = sb("st_row", [P, 2, E_ST], I32, regions)
        st_ohT = sb("st_ohT", [P, 2, 2, P], F32, regions)
        st_ohTr = sb("st_ohTr", [P, 2, 2, 2, P], F32R, regions)
        st_scl = sb("st_scl", [P, N], BF16, regions)
        st_one = sb("st_one", [P, N], BF16, regions)
        st_scr = sb("st_scr", [P, 3, N], BF16, regions)
        sort = ExitStack()
        edges = sb("edges", [P, 2, JH], I32, sort)
        e_i = sb("e_i", [P, 2, 2, JH], I32, sort)
        cls = sb("cls", [P, JH], F32, sort)
        val = sb("val", [P, 2, JH], BF16, sort)
        tot = sb("tot", [P, NC], BF16, sort)
        cw = sb("cw", [P, 6, NC], F32, sort)
        cwi = sb("cwi", [P, 2, NC], I32, sort)
        slot = sb("slot", [P, JH], F32, sort)
        slot_i = sb("slot_i", [P, 3, JH], I32, sort)
        slot_f = sb("slot_f", [P, 2, JH], F32, sort)
        pos_oh = sb("pos_oh", [P, JS, P], BF16, sort)
        tile_oh = sb("tile_oh", [P, JS, NT], BF16, sort)
        cle = sb("cle", [P, NT, NC], BF16, sort)
        tcls = sb("tcls", [P, 2, NT], F32, sort)
        tcls_i = sb("tcls_i", [P, 5, NT], I32, sort)
        key_col = sb("key_col", [P, 2, NT], F32, sort)
        key_u8 = sb("key_u8", [NT, 2, P], U8, sort)
        ranks = ExitStack()
        cls_oh = sb("cls_oh", [P, NC, JH], F32, ranks)
        gate = sb("gate", [P, NC, JH], F32, ranks)
        cum = sb("cum", [P, NC, JH], F32, ranks)
        ranks.close()
        tile_val = sb("tile_val", [P, JS, 2, NT], BF16, sort)
        sort.close()
        key_rows = sb("key_rows", [P, 2, NT * P], U8, regions)
        x_both = sb("x_both", [P, KC, 2, 2, Q], F32R, regions)
        regions.close()
        last = ExitStack()
        PT = sb("PT", [P, 2, N], F32, last)
        zT_hi = sb("zT_hi", [P, KC, N], F32R, last)
        zT_lo = sb("zT_lo", [P, KC, N], F32R, last)
        z_both = sb("z_both", [P, KC, 2, 2, Q], F32R, last)
        bn_bc = sb("bn_bc", [P, 2, D], F32, last)
        x1 = sb("x1", [P, 2, D], F32, last)
        h1 = sb("h1", [P, 2, D], F32, last)
        y1 = sb("y1", [P, 2, D], F32, last)
        y2 = sb("y2", [P, 2, D], F32, last)
        last.close()
        soft = junk[:, 0, :].bitcast(F32)

        key_dram = nc.dram_tensor("key_rows_scratch", [2, NT, P], U8, kind="Internal").ap()

        ps = ctx.enter_context(nc.psum_tensor("ps", [P, 4096], F32))
        G0, G1 = ps[:, 0:2048], ps[:, 2048:4096]

        def flat(T, a=0, b=KC):
            return T[:, a:b, :].rearrange("p c n -> p (c n)")

        def bank(b):
            return ps[:, b * 512:(b + 1) * 512]

        x_in = sem("x_in")
        edges_in = sem("edges_in")
        st_rows_in = sem("st_rows_in")
        consts_in = sem("consts_in")
        biases_in = sem("biases_in")
        w_in = [sem(f"w_in{i}") for i in range(NS)]
        hi_made = sem("hi_made")
        lo_made = sem("lo_made")
        lo_pool = sem("lo_pool")
        chunk_used = sem("chunk_used")
        pool_done = sem("pool_done")
        dve_done = sem("dve_done")
        setup_done = sem("setup_done")
        pe_step = sem("pe_step")
        act_step = sem("act_step")
        dve_step = sem("dve_step")
        placed = sem("placed")
        keys_out = sem("keys_out")
        keys_back = sem("keys_back")
        st_oh = sem("st_oh")
        st_made = sem("st_made")
        dist_made = sem("dist_made")
        oh_made = sem("oh_made")
        keys_staged = sem("keys_staged")
        gathered = sem("gathered")
        reduced = sem("reduced")
        ones_made = sem("ones_made")
        sc_made = sem("sc_made")
        scattered = sem("scattered")
        both_made = sem("both_made")
        out_in = sem("out_in")

        stream = [("hh", W_hh, k) for k in range(0, 2 * KC, 2)]
        stream += [("oo", W_oo, k) for k in range(0, 2 * KC, 2)]
        stream += [("ho", W_ho, k) for k in range(0, 2 * KC, 2)]
        for k in range(0, 2 * KC, 2):
            stream += [("hn", W_hn, k), ("on", W_on, k)]
        stream += [("l1", L1_W, k) for k in range(0, KC, 2)]
        chunks = [(name, k + i) for name, _, k in stream for i in range(2)]
        turn = {key: n for n, key in enumerate(chunks)}
        END = {"hh": 16, "ooA": 24, "ooB": 32, "hoA": 40, "hoB": 48, "updx": 64, "upd": 80, "h1": 88}

        UX = END["hoB"] + 12

        def by_pool(n):
            return n >= END["hoB"] + NB and n % 4 == 3

        def lo_count(n, pool):
            return sum(by_pool(m) == pool for m in range(n + 1))

        PE_STAGES = ["xT", "ghT", "totals", "perm0", "perm1", "keysT", "PT", "zT0", "zT1", "x1T", "albc", "hp"]
        ACT_STAGES = ["xT", "ghT", "ooA_hi", "ooB_hi", "hoA_hi", "hoB_hi", "soft", "zT0", "zT1", "lows", "sd0", "x1T",
                      "h1_0", "h1_1", "lrelu", "elu", "sd1"]
        DVE_STAGES = ["tot", "xT", "ghT", "slots", "tiles0", "steer", "D_hh", "ooA_b", "ooA_lo", "ooB_lo", "key0",
                      "tiles1", "D_oo", "keys", "key_u8", "hoA_b", "hoA_lo", "hoB_lo", "maxima", "P", "PT", "zT0",
                      "zT1", "var0", "x1", "x1T", "al", "lr", "ET", "hpn", "var1", "out"]

        def pe_at(s):
            return PE_STAGES.index(s) + 1

        def act_at(s):
            return ACT_STAGES.index(s) + 1

        def dve_at(s):
            return DVE_STAGES.index(s) + 1

        block = ctx.enter_context(nc.Block())

        @block.sync
        def _(sp):
            sp.dma_start(x_nat[:], x.rearrange("(h p) d -> p h d", p=P)).then_inc(x_in, 16)
            for n, (name, W, k) in enumerate(stream):
                if n >= NS:
                    last_of = 2 * (n - NS) + 1
                    sp.wait_ge(lo_made, lo_count(last_of, False))
                    if lo_count(last_of, True):
                        sp.wait_ge(lo_pool, lo_count(last_of, True))
                sp.dma_start(W_raw[:, n % NS, :, :], W[k * P:(k + 2) * P, :].rearrange("(i p) d -> p i d", p=P)) \
                  .then_inc(w_in[n % NS], 16)
            sp.wait_ge(dve_step, dve_at("out"))
            sp.dma_start(out.rearrange("(h p) d -> p h d", p=P), y2[:]).then_inc(out_in, 16)
            sp.wait_ge(out_in, 16)

        @block.gpsimd
        def _(pool):
            mine = [0]

            def link(ins):
                mine[0] += 1
                ins.then_inc(pool_done, 1)
                pool.wait_ge(pool_done, mine[0])

            ga = nc.gpsimd
            exact = dict(allow_small_or_imprecise_dtypes=True)
            ga.memset(gate[:], 1.0).then_inc(pool_done, 1)
            ga.iota(irow[:], pattern=[[1, N + 1]], base=0, channel_multiplier=0, **exact).then_inc(pool_done, 1)
            ga.memset(ident[:], 0.0).then_inc(pool_done, 1)
            for h in range(2):
                ga.iota(pcol[:, 1 + h:2 + h], pattern=[[0, 1]], base=h * P, channel_multiplier=1, **exact) \
                  .then_inc(pool_done, 1)
            ga.memset(tri[:], 1.0).then_inc(pool_done, 1)
            ga.memset(ones_b[:], 1.0).then_inc(pool_done, 1)
            ga.memset(ones_f[:], 1.0).then_inc(pool_done, 1)
            ga.memset(zero_b[:], 0.0).then_inc(pool_done, 1)
            ga.memset(spare[:], 0.0).then_inc(pool_done, 1)
            ga.memset(eps_ln[:], EPS_LN).then_inc(pool_done, 1)
            pool.wait_ge(pool_done, 11)
            mine[0] = 11
            link(ga.affine_select(out=ident[:], in_=ident[:], compare_op=ALU.not_equal, fill=1.0, base=0,
                                  pattern=[[-1, P]], channel_multiplier=1))
            link(ga.affine_select(out=tri[:], in_=tri[:], compare_op=ALU.is_gt, fill=0.0, base=0,
                                  pattern=[[1, P]], channel_multiplier=-1))
            link(ga.memset(gate[:, :, 0:1], 0.0))
            for q in range(2):
                link(ga.iota(pcol[q * Q:(q + 1) * Q, 0:1], pattern=[[0, 1]], base=1, channel_multiplier=1, **exact))
            link(ga.tensor_scalar(pcol[:, 3:4], pcol[:, 0:1], -1.0, None, ALU.mult))
            ga.nop().then_inc(setup_done, 1)

            pool.wait_ge(st_rows_in, 32)
            for k in range(2):
                for h in range(2):
                    ga.tensor_scalar(st_ohT[:, k, h, :], st_row[:, k, 0:P], pcol[:, 1 + h:2 + h], None,
                                     ALU.is_equal).then_inc(st_oh, 1)

            def oo_onehots(t):
                if t >= 3:
                    pool.wait_ge(gathered, t - 2)
                for k in range(2):
                    edges_of = st_row[:, k, E_HH:E_ST].rearrange("p (m t) -> p t m", t=JO)[:, t - 1, :]
                    for h in range(2):
                        ga.tensor_scalar(st_ohTr[:, t % 2, k, h, :], edges_of, pcol[:, 1 + h:2 + h], None,
                                         ALU.is_equal).then_inc(st_oh, 1)

            def place(s):
                cols = slice(s * JS, (s + 1) * JS)
                if s == 0:
                    pool.wait_ge(dve_step, dve_at("slots"))
                else:
                    pool.wait_ge(pe_step, pe_at("perm0"))
                link(ga.tensor_tensor(pos_oh[:], slot_f[:, 1, cols].unsqueeze(2).broadcast_to([P, JS, P]),
                                      irow[:, 0:P].unsqueeze(1).broadcast_to([P, JS, P]), ALU.subtract))
                link(ga.tensor_scalar(pos_oh[:], pos_oh[:], 0.0, None, ALU.is_equal))
                pool.wait_ge(dve_step, dve_at(f"tiles{s}"))
                for k in range(2):
                    ins = ga.tensor_tensor(tile_val[:, :, k, :], tile_oh[:],
                                           val[:, k, cols].unsqueeze(2).broadcast_to([P, JS, NT]), ALU.mult)
                    link(ins)
                ga.nop().then_inc(placed, 1)

            oo_onehots(1)
            oo_onehots(2)
            place(0)
            oo_onehots(3)
            oo_onehots(4)
            oo_onehots(5)
            place(1)

            def settle(n):
                ga.tensor_tensor(spare[0:1, n:n + 1], zero_b[0:1, 0:1], zero_b[0:1, 1:2], ALU.add)

            def ho_turn(i):
                first = isinstance(i, int)
                if not first:
                    pool.wait_ge(sc_made, 2 * U * i)
                    settle(0)
                ga.tensor_copy(keys_now[:], keys[:, 0:U, :] if first else keys[:, bass.ds(U * i, U), :]) \
                  .then_inc(keys_staged, 1)
                pool.wait_ge(keys_staged, i + 1)
                for b in range(U):
                    if not first:
                        pool.wait_ge(scattered, 1 + JO + U * i + b - U + 1)
                    pool.wait_ge(reduced, 1 + JO + U * i + b + 1)
                    if not first:
                        settle(1 + b)
                    ga.tensor_scalar(sc_r[:, b, 0, :], irow[:, 1:Q + 1], keys_now[:, b, 0:1],
                                     logit_now[:, b:b + 1], ALU.is_equal, ALU.mult).then_inc(sc_made, 1)
                    ga.tensor_scalar(sc_l[:, b, :], irow[:, 1:P + 1], keys_now[:, b, 1:2], None,
                                     ALU.is_equal).then_inc(sc_made, 1)

            def side_by_side(both, hi, lo, a, b):
                for q in range(2):
                    for i, part in enumerate((hi, lo) if q == 0 else (lo, hi)):
                        ins = ga.tensor_copy(both[:, a:b, q, i, :], part[:, a:b, q * Q:(q + 1) * Q])
                        if (q, i) != (1, 1):
                            link(ins)
                ins.then_inc(both_made, 1)

            pool.wait_ge(keys_out, 16)
            side_by_side(x_both, xT_hi, xT_lo, 0, KC)
            ho_turn(0)
            with pool.Fori(1, TURNS) as i:
                ho_turn(i)

            def lows(a, b):
                for n in range(a, b):
                    if by_pool(n):
                        pool.wait_ge(hi_made, n + 1)
                        ga.tensor_tensor(W_lo[:, n % NB, :], W_raw[:, n // 2 % NS, n % 2, :],
                                         W_hi[:, n % NB, :].bitcast(F32), ALU.subtract).then_inc(lo_pool, 1)

            lows(0, UX)
            for s in range(2):
                pool.wait_ge(dve_step, dve_at(f"zT{s}"))
                side_by_side(z_both, zT_hi, zT_lo, 4 * s, 4 * s + 4)
                lows(UX + 2 * s, UX + 2 * s + 2)
            lows(UX + 4, len(chunks))

        @block.scalar
        def _(act):
            sa = nc.scalar
            for k, v in enumerate((src, dst)):
                act.dma_start(edges[:, k, :], v[E_ST:E].rearrange("(p j) -> p j", p=P)).then_inc(edges_in, 16)
            for k, v in enumerate((src, dst)):
                act.dma_start(st_row[:, k, :], v[0:E_ST].partition_broadcast(P)).then_inc(st_rows_in, 16)
            for k, v in enumerate((src, dst)):
                act.dma_start(st_col[:, k, 0:1], v[0:E_HH].rearrange("(p j) -> p j", p=P)).then_inc(consts_in, 16)
                act.dma_start(st_col[:, k, 1:], v[E_HH:E_ST].rearrange("(p j) -> p j", p=P)).then_inc(consts_in, 16)
            act.dma_start(wa_bc[:], W_a.rearrange("d o -> (d o)").partition_broadcast(P)).then_inc(consts_in, 16)
            act.dma_start(ba_bc[:], b_a.partition_broadcast(P)).then_inc(consts_in, 16)
            act.dma_start(bias_bc[:, 0, :], b_hh.partition_broadcast(P)).then_inc(biases_in, 16)
            act.dma_start(bias_bc[:, 1, :], b_oo.partition_broadcast(P)).then_inc(biases_in, 16)

            def high(n):
                act.wait_ge(w_in[n // 2 % NS], 16 * (n // 2 // NS + 1))
                if n >= NB:
                    act.wait_ge(chunk_used, n - NB + 1)
                sa.copy(W_hi[:, n % NB, :], W_raw[:, n // 2 % NS, n % 2, :]).then_inc(hi_made, 1)

            def highs(a, b):
                for n in range(a + NB if a else 0, min(b + NB, len(chunks))):
                    high(n)

            act.wait_ge(pe_step, pe_at("xT"))
            sa.copy(flat(xT_hi), G0).then_inc(act_step, 1)
            act.wait_ge(pe_step, pe_at("ghT"))
            sa.copy(hh_hi.rearrange("p a c n -> p (a c n)"), G1).then_inc(act_step, 1)
            highs(0, END["ooA"])
            act.wait_ge(dve_step, dve_at("ooA_b"))
            sa.copy(Ao_tab[:, :, 0, :], G1.rearrange("p (h d) -> p h d", h=2)).then_inc(act_step, 1)
            highs(END["ooA"], END["ooB"])
            act.wait_ge(chunk_used, END["ooB"])
            sa.copy(Bo_tab[:, :, 0, :], G0.rearrange("p (h d) -> p h d", h=2)).then_inc(act_step, 1)
            act.wait_ge(dve_step, dve_at("D_hh"))
            act.dma_start(bias_bc[:, 0, :], b_ho.partition_broadcast(P)).then_inc(biases_in, 16)
            highs(END["ooB"], END["hoA"])
            act.wait_ge(dve_step, dve_at("key_u8"))
            act.dma_start(key_dram.rearrange("k t m -> t k m"), key_u8[:]).then_inc(keys_out, 16)

            def table_high(tab, acc):
                for q in range(4):
                    r = (q % 2) * Q
                    ins = sa.copy(tab[0:Q, q, :], acc[r:r + Q, (q // 2) * D:(q // 2 + 1) * D])
                ins.then_inc(act_step, 1)

            act.wait_ge(dve_step, dve_at("hoA_b"))
            table_high(A_tab, G1)
            act.wait_ge(keys_out, 16)
            act.dma_start(key_rows[:].rearrange("p k n -> p (k n)"),
                          key_dram.rearrange("k t m -> (k t m)").partition_broadcast(P)).then_inc(keys_back, 16)
            for k in range(2):
                act.dma_start(bias_bc[:, k, :], L1_a[0, k * D:(k + 1) * D].partition_broadcast(P)) \
                   .then_inc(biases_in, 16)
            highs(END["hoA"], END["hoB"])
            act.wait_ge(chunk_used, END["hoB"])
            table_high(B_tab, G0)

            def distance(t, b):
                k = key_rows[:, :, t * P:(t + 1) * P] if isinstance(t, int) else key_rows[:, :, bass.ds(t * P, P)]
                sa.activation(oh_dist[:, b, :, :], k, ACT.Abs, bias=pcol[:, 3:4]).then_inc(dist_made, 1)

            def onehot(t, b):
                act.wait_ge(dist_made, t + 1)
                if not isinstance(t, int) or t >= 1:
                    act.wait_ge(oh_made, t)
                    act.wait_ge(gathered, JO + t - 1)
                sa.activation(oh[:, b, :, :], oh_dist[:, b, :, :], ACT.Relu, bias=1.0, scale=-1.0) \
                  .then_inc(oh_made, 1)

            act.wait_ge(keys_back, 16)
            distance(0, 0)
            onehot(0, 0)
            distance(1, 1)
            with act.Fori(1, NT // 2) as i:
                onehot(2 * i - 1, 1)
                distance(2 * i, 0)
                onehot(2 * i, 0)
                distance(2 * i + 1, 1)
            onehot(NT - 1, 1)

            act.wait_ge(gathered, JO + NT)
            act.dma_start(bn_bc[0:Q, 0, :], b_hn.partition_broadcast(Q)).then_inc(biases_in, 16)
            act.dma_start(bn_bc[Q:P, 0, :], b_on.partition_broadcast(Q)).then_inc(biases_in, 16)
            act.dma_start(bn_bc[:, 1, :], b_on.partition_broadcast(P)).then_inc(biases_in, 16)
            highs(END["hoB"], UX - NB)
            act.wait_ge(dve_step, dve_at("maxima"))
            for h in range(2):
                ins = sa.activation(S_log[:, :, h, :], S_log[:, :, h, :], ACT.Exp, bias=small[:, h:h + 1])
            ins.then_inc(act_step, 1)
            highs(UX - NB, UX)
            for s in range(2):
                act.wait_ge(pe_step, pe_at(f"zT{s}"))
                sa.copy(flat(zT_hi, 4 * s, 4 * s + 4), G0[:, 0:D]).then_inc(act_step, 1)
                highs(UX + 2 * s, UX + 2 * s + 2)
            highs(UX + 4, END["upd"])
            act.wait_ge(chunk_used, END["upd"])
            sa.copy(y2[0:Q, 0, :], G0[Q:P, D:2 * D])
            sa.copy(y2[Q:P, 0, :], G1[0:Q, 0:D]).then_inc(act_step, 1)
            act.wait_ge(dve_step, dve_at("var0"))
            sa.activation(small[:, 8:10], small[:, 4:6], ACT.Sqrt, bias=eps_ln[:, 0:1]).then_inc(act_step, 1)
            act.wait_ge(pe_step, pe_at("x1T"))
            sa.copy(flat(xT_hi), G0).then_inc(act_step, 1)
            highs(END["upd"], END["h1"])
            act.wait_ge(chunk_used, END["h1"])
            for h in range(2):
                sa.copy(h1[:, h, :], G1[:, h * D:(h + 1) * D]).then_inc(act_step, 1)
            act.wait_ge(dve_step, dve_at("lr"))
            sa.activation(PT[:], PT[:], ACT.Exp, scale=-1.0).then_inc(act_step, 1)
            act.wait_ge(dve_step, dve_at("hpn"))
            sa.activation(y2[:], y2[:], ACT.Exp).then_inc(act_step, 1)
            act.wait_ge(dve_step, dve_at("var1"))
            sa.activation(small[:, 8:10], small[:, 4:6], ACT.Sqrt, bias=eps_ln[:, 0:1]).then_inc(act_step, 1)

        @block.vector
        def _(dve):
            v = nc.vector
            mine = [0]

            def link(ins):
                mine[0] += 1
                ins.then_inc(dve_done, 1)
                dve.wait_ge(dve_done, mine[0])

            said = [0]

            def stage(name):
                assert DVE_STAGES[said[0]] == name, name
                said[0] += 1
                v.nop().then_inc(dve_step, 1)

            def low(n):
                if not by_pool(n):
                    dve.wait_ge(hi_made, n + 1)
                    v.tensor_tensor(W_lo[:, n % NB, :], W_raw[:, n // 2 % NS, n % 2, :],
                                    W_hi[:, n % NB, :].bitcast(F32), ALU.subtract).then_inc(lo_made, 1)

            def lows(a, b):
                for n in range(a, b):
                    low(n)

            dve.wait_ge(edges_in, 32)
            link(v.tensor_scalar(e_i[:, 0, :, :], edges[:], 6, None, ALU.logical_shift_right))
            link(v.tensor_scalar(e_i[:, 1, :, :], edges[:], Q - 1, None, ALU.bitwise_and))
            link(v.scalar_tensor_tensor(cls[:], e_i[:, 0, 0, :], 4.0, e_i[:, 0, 1, :], ALU.mult, ALU.add))
            link(v.tensor_scalar(val[:], e_i[:, 1, :, :], 1.0, None, ALU.add))
            dve.wait_ge(setup_done, 1)
            link(v.tensor_tensor(cls_oh[:], cls[:].unsqueeze(1).broadcast_to([P, NC, JH]),
                                 irow[:, 0:NC].unsqueeze(2).broadcast_to([P, NC, JH]), ALU.is_equal))
            link(v.tensor_tensor_scan(cum[:].rearrange("p c j -> p (c j)"), gate[:].rearrange("p c j -> p (c j)"),
                                      cls_oh[:].rearrange("p c j -> p (c j)"), 0.0, ALU.mult, ALU.add))
            link(v.tensor_copy(tot[:], cum[:, :, JH - 1]))
            stage("tot")
            dve.wait_ge(act_step, act_at("xT"))
            link(v.tensor_tensor(flat(xT_lo), G0, flat(xT_hi).bitcast(F32), ALU.subtract))
            stage("xT")
            dve.wait_ge(act_step, act_at("ghT"))
            link(v.tensor_tensor(hh_lo.rearrange("p a c n -> p (a c n)"), G1,
                                 hh_hi.rearrange("p a c n -> p (a c n)").bitcast(F32), ALU.subtract))
            stage("ghT")
            lows(0, NB)

            dve.wait_ge(pe_step, pe_at("totals"))
            pre, allc = bank(2)[:, 0:NC], bank(2)[:, NC:2 * NC]
            link(v.tensor_scalar(cwi[:, 0, :], allc, float(P - 1), None, ALU.add))
            link(v.tensor_scalar(cwi[:, 1, :], cwi[:, 0, :], 7, None, ALU.logical_shift_right))
            link(v.tensor_copy(cw[:, 0, :], cwi[:, 1, :]))
            link(v.memset(cw[:, 5, :], 1.0))
            link(v.tensor_tensor_scan(cw[:, 1, :], cw[:, 5, :], cw[:, 0, :], 0.0, ALU.mult, ALU.add))
            link(v.tensor_tensor(cw[:, 2, :], cw[:, 1, :], cw[:, 0, :], ALU.subtract))
            link(v.tensor_scalar(cw[:, 3, :], cw[:, 2, :], float(P), -1.0, ALU.mult, ALU.add))
            link(v.tensor_tensor(cw[:, 4, :], cw[:, 3, :], pre, ALU.add))
            low(NB)
            link(v.tensor_tensor(cum[:], cum[:], cw[:, 4, :].unsqueeze(2).broadcast_to([P, NC, JH]), ALU.add))
            link(v.tensor_tensor(cum[:], cum[:], cls_oh[:], ALU.mult))
            low(NB + 1)
            link(v.tensor_reduce(slot[:], cum[:].rearrange("p c j -> p j c"), AX, ALU.add))
            link(v.tensor_copy(slot_i[:, 0, :], slot[:]))
            link(v.tensor_scalar(slot_i[:, 1, :], slot_i[:, 0, :], 7, None, ALU.logical_shift_right))
            link(v.tensor_scalar(slot_i[:, 2, :], slot_i[:, 0, :], P - 1, None, ALU.bitwise_and))
            link(v.tensor_copy(slot_f[:], slot_i[:, 1:3, :]))
            stage("slots")
            lows(NB + 2, END["hh"] + NB)

            def tiles(s):
                link(v.tensor_tensor(tile_oh[:], slot_f[:, 0, s * JS:(s + 1) * JS].unsqueeze(2)
                                     .broadcast_to([P, JS, NT]), irow[:, 0:NT].unsqueeze(1)
                                     .broadcast_to([P, JS, NT]), ALU.is_equal))
                stage(f"tiles{s}")

            def static_tile(t):
                if t == 0:
                    acc = G0[:, 0:D]
                    dve.wait_ge(chunk_used, END["hh"])
                    dve.wait_ge(biases_in, 32)
                    dve.wait_ge(consts_in, 96)
                    link(v.tensor_copy(st_colf[:], st_col[:]))
                    link(v.tensor_tensor(acc, acc, bias_bc[:, 0, :], ALU.add))
                else:
                    acc = G1[:, (t % 2) * D:(t % 2 + 1) * D]
                    dve.wait_ge(gathered, t)
                link(v.scalar_tensor_tensor(junk[:, 0, :], acc, 0.0, wa_bc[:], ALU.max, ALU.mult,
                                            accum_out=st_logit[:, t:t + 1]))
                v.nop().then_inc(reduced, 1)
                if t >= 1:
                    dve.wait_ge(scattered, t)
                link(v.tensor_copy(part_b[:, 0:1], st_logit[:, t:t + 1]))
                link(v.tensor_tensor(part_f[:, 0:1], st_logit[:, t:t + 1], part_b[:, 0:1], ALU.subtract))
                link(v.tensor_copy(part_b[:, 1:2], part_f[:, 0:1]))
                link(v.tensor_tensor(part_f[:, 1:2], part_f[:, 0:1], part_b[:, 1:2], ALU.subtract))
                link(v.tensor_copy(small[:, 60:61], part_b[:, 0:1]))
                link(v.tensor_copy(small[:, 61:62], part_b[:, 1:2]))
                link(v.tensor_copy(small[:, 62:63], part_f[:, 1:2]))
                link(v.tensor_scalar(st_scl[:], irow[:, 0:N], st_colf[:, 1, t:t + 1], None, ALU.is_equal))
                link(v.tensor_scalar(st_one[:], irow[:, 0:N], st_colf[:, 0, t:t + 1], None, ALU.is_equal))
                for r in range(3):
                    ins = v.tensor_scalar(st_scr[:, r, :], st_one[:], small[:, 60 + r:61 + r], None, ALU.mult)
                    link(ins)
                v.nop().then_inc(st_made, 1)

            def take_sums(kind, banks):
                C, L = S_cnt[:, kind, :, :], S_log[:, kind, :, :]
                Cf, Lf = C.rearrange("p h n -> p (h n)"), L.rearrange("p h n -> p (h n)")
                link(v.tensor_copy(Cf, bank(banks[1])))
                link(v.tensor_scalar(soft, Cf, 1.0, None, ALU.max))
                link(v.reciprocal(soft, soft))
                link(v.tensor_tensor(Lf, bank(banks[0]), soft, ALU.mult))
                link(v.tensor_scalar(soft, Cf, 0.0, -BIG, ALU.is_equal, ALU.mult))
                link(v.scalar_tensor_tensor(Lf, Lf, ba_bc[:, 0:1], soft, ALU.add, ALU.add))

            static_tile(0)
            low(END["hh"] + NB)
            link(v.tensor_tensor(cle[:], cw[:, 1, :].unsqueeze(1).broadcast_to([P, NT, NC]),
                                 irow[:, 0:NT].unsqueeze(2).broadcast_to([P, NT, NC]), ALU.is_le))
            low(END["hh"] + NB + 1)
            tiles(0)
            low(END["hh"] + NB + 2)
            link(v.tensor_reduce(tcls[:, 0, :], cle[:], AX, ALU.add))
            link(v.tensor_scalar(tcls_i[:, 0, :], tcls[:, 0, :], float(NC - 1), None, ALU.min))
            link(v.tensor_scalar(tcls_i[:, 1, :], tcls_i[:, 0, :], 2, None, ALU.logical_shift_right))
            link(v.tensor_scalar(tcls_i[:, 2, :], tcls_i[:, 0, :], 3, None, ALU.bitwise_and))
            link(v.tensor_scalar(tcls_i[:, 3, :], tcls_i[:, 2, :], 1, None, ALU.bitwise_and))
            link(v.tensor_scalar(tcls_i[:, 4, :], tcls_i[:, 2, :], 1, None, ALU.logical_shift_right))
            low(END["hh"] + NB + 3)
            link(v.scalar_tensor_tensor(tcls_i[:, 0, :], tcls_i[:, 4, :], 4.0, tcls_i[:, 1, :], ALU.mult, ALU.add))
            link(v.memset(steer[:], 0))
            for c in range(2):
                link(v.tensor_copy(steer[0:1, 0:TURNS, c, :], tcls_i[0:1, 1 + c, :].rearrange("p (i b) -> p i b", b=U)))
            blocks = tcls_i[0:1, 0, :].rearrange("p (i b) -> p i b", b=U)
            link(v.tensor_copy(steer[0:1, 1:TURNS + 1, 2, :], blocks))
            link(v.tensor_scalar(tcls[:, 1, :], tcls_i[:, 3, :], float(Q), None, ALU.mult))
            stage("steer")
            lows(END["hh"] + NB + 4, END["ooA"] + NB)

            def add_bias(acc, k):
                for h in range(2):
                    link(v.tensor_tensor(acc[:, h * D:(h + 1) * D], acc[:, h * D:(h + 1) * D], bias_bc[:, k, :],
                                         ALU.add))

            def low_half(tab, acc):
                for h in range(2):
                    link(v.tensor_tensor(tab[:, h, 1, :], acc[:, h * D:(h + 1) * D],
                                         tab[:, h, 0, :].bitcast(F32), ALU.subtract))

            def low_quarter(tab, acc):
                for q in range(4):
                    r = (q % 2) * Q
                    link(v.tensor_tensor(tab[Q:P, q, :], acc[r:r + Q, (q // 2) * D:(q // 2 + 1) * D],
                                         tab[0:Q, q, :].bitcast(F32), ALU.subtract))

            dve.wait_ge(scattered, 1)
            take_sums(0, (2, 3))
            stage("D_hh")
            dve.wait_ge(chunk_used, END["ooA"])
            add_bias(G1, 1)
            stage("ooA_b")
            low(END["ooA"] + NB)
            dve.wait_ge(act_step, act_at("ooA_hi"))
            low_half(Ao_tab, G1)
            stage("ooA_lo")
            lows(END["ooA"] + NB + 1, END["ooB"] + NB)
            dve.wait_ge(act_step, act_at("ooB_hi"))
            low_half(Bo_tab, G0)
            stage("ooB_lo")
            dve.wait_ge(pe_step, pe_at("perm0"))
            link(v.tensor_copy(key_col[:].rearrange("p k t -> p (k t)"), bank(4)[:, 0:2 * NT]))
            stage("key0")
            tiles(1)
            for t in range(1, 1 + JO):
                static_tile(t)
            low(END["ooB"] + NB)
            low(END["ooB"] + NB + 1)
            lows(END["ooB"] + NB + 2, END["hoA"] + NB)
            dve.wait_ge(scattered, 1 + JO)
            take_sums(1, (0, 1))
            stage("D_oo")
            for h in range(2):
                link(v.tensor_reduce(top[:, 0, h:h + 1], S_log[:, 0:2, h, :], AXY, ALU.max))
            dve.wait_ge(pe_step, pe_at("perm1"))
            link(v.tensor_tensor(key_col[:].rearrange("p k t -> p (k t)"), key_col[:].rearrange("p k t -> p (k t)"),
                                 bank(3)[:, 0:2 * NT], ALU.add))
            link(v.tensor_copy(keys[:, :, 0], key_col[:, 0, :]))
            link(v.tensor_tensor(keys[:, :, 1], key_col[:, 1, :], tcls[:, 1, :], ALU.add))
            stage("keys")
            dve.wait_ge(pe_step, pe_at("keysT"))
            link(v.tensor_copy(key_u8[:].rearrange("t k m -> t (k m)"), bank(2)[0:NT, 0:2 * P]))
            stage("key_u8")
            dve.wait_ge(biases_in, 48)
            dve.wait_ge(chunk_used, END["hoA"])
            add_bias(G1, 0)
            stage("hoA_b")
            low(END["hoA"] + NB)
            dve.wait_ge(act_step, act_at("hoA_hi"))
            low_quarter(A_tab, G1)
            stage("hoA_lo")
            lows(END["hoA"] + NB + 1, END["hoB"] + NB)
            dve.wait_ge(act_step, act_at("hoB_hi"))
            low_quarter(B_tab, G0)
            stage("hoB_lo")

            def edge_tile(t, b):
                first = isinstance(t, int)
                acc = G1[:, (b % 2) * D:(b % 2 + 1) * D]
                if not first:
                    dve.wait_ge(sc_made, 2 * (t - U + 1))
                dve.wait_ge(gathered, JO + 1 + t)
                v.scalar_tensor_tensor(junk[:, b % 2, :], acc, 0.0, wa_bc[:], ALU.max, ALU.mult,
                                       accum_out=logit_now[:, b:b + 1]).then_inc(reduced, 1)
                if not first:
                    dve.wait_ge(scattered, 1 + JO + t - U + 1)
                v.tensor_scalar(sc_r[:, b, 1, :], irow[:, 1:Q + 1], keys[:, t:t + 1, 0] if first else
                                keys[:, bass.ds(t, 1), 0], None, ALU.is_equal).then_inc(ones_made, 1)

            for b in range(U):
                edge_tile(b, b)
            with dve.Fori(1, TURNS) as i:
                for b in range(U):
                    edge_tile(U * i + b, b)
            dve.wait_ge(reduced, 1 + JO + NT)

            lows(END["hoB"] + NB, END["hoB"] + NB + 3)
            dve.wait_ge(scattered, 1 + JO + NT)
            take_sums(2, (0, 1))
            lows(END["hoB"] + NB + 3, END["hoB"] + NB + 6)
            link(v.tensor_reduce(top[:, 1, :], S_log[:, 2, :, :], AX, ALU.max))
            link(v.tensor_tensor(small[:, 2:4], top[:, 0, :], top[:, 1, :], ALU.max))
            link(v.tensor_scalar(small[:, 0:2], small[:, 2:4], -1.0, None, ALU.mult))
            stage("maxima")
            lows(END["hoB"] + NB + 6, UX)
            dve.wait_ge(act_step, act_at("soft"))
            Lf, Cf = S_log[:].rearrange("p k h n -> p (k h n)"), S_cnt[:].rearrange("p k h n -> p (k h n)")
            link(v.tensor_tensor(Lf, Lf, Cf, ALU.mult))
            link(v.tensor_tensor(S_log[:, 0, :, :], S_log[:, 0, :, :], S_log[:, 1, :, :], ALU.add))
            link(v.tensor_tensor(S_log[:, 0, :, :], S_log[:, 0, :, :], S_log[:, 2, :, :], ALU.add))
            link(v.tensor_reduce(small[:, 4:6], S_log[:, 0, :, :], AX, ALU.add))
            link(v.tensor_scalar(small[:, 6:8], small[:, 4:6], 0.0, None, ALU.is_equal))
            link(v.tensor_tensor(small[:, 4:6], small[:, 4:6], small[:, 6:8], ALU.add))
            link(v.reciprocal(small[:, 6:8], small[:, 4:6]))
            for h in range(2):
                link(v.tensor_scalar(S_log[:, 0, h, :], S_log[:, 0, h, :], small[:, 6 + h:7 + h], None, ALU.mult))
            stage("P")
            lows(UX, UX + NB)
            dve.wait_ge(pe_step, pe_at("PT"))
            link(v.tensor_copy(PT[:].rearrange("p h n -> p (h n)"), bank(0)))
            stage("PT")
            for s in range(2):
                dve.wait_ge(act_step, act_at(f"zT{s}"))
                own = (4 * s, 4 * s + 4)
                link(v.tensor_tensor(flat(zT_lo, *own), G0[:, 0:D], flat(zT_hi, *own).bitcast(F32), ALU.subtract))
                stage(f"zT{s}")
                lows(UX + NB + 2 * s, UX + NB + 2 * s + 2)
            lows(UX + NB + 4, END["upd"] + NB)
            link(v.tensor_tensor(S_cnt[:, 0, :, :], S_cnt[:, 0, :, :], S_cnt[:, 1, :, :], ALU.add))
            link(v.tensor_tensor(S_cnt[:, 0, :, :], S_cnt[:, 0, :, :], S_cnt[:, 2, :, :], ALU.add))

            def statistics(res, h):
                for g in range(2):
                    link(v.bn_stats(small[:, 16 + 12 * h + 6 * g:22 + 12 * h + 6 * g],
                                    res[:, h, g * 512:(g + 1) * 512]))
                link(v.bn_aggr(small[:, 40 + 2 * h:42 + 2 * h], small[:, 16 + 12 * h:28 + 12 * h]))
                link(v.tensor_copy(small[:, 4 + h:5 + h], small[:, 41 + 2 * h:42 + 2 * h]))

            def normalise(res, dest, deviation):
                dve.wait_ge(act_step, act_at(deviation))
                link(v.reciprocal(small[:, 10:12], small[:, 8:10]))
                for h in range(2):
                    link(v.tensor_scalar(dest[:, h, :], res[:, h, :], small[:, 40 + 2 * h:41 + 2 * h],
                                         small[:, 10 + h:11 + h], ALU.subtract, ALU.mult))

            dve.wait_ge(biases_in, 128)
            dve.wait_ge(chunk_used, END["upd"])
            link(v.tensor_tensor(y1[:, 1, :], G1[:, D:2 * D], bn_bc[:, 1, :], ALU.add))
            link(v.scalar_tensor_tensor(y1[:, 1, :], y1[:, 1, :], 0.0, x_nat[:, 1, :], ALU.max, ALU.add))
            statistics(y1, 1)
            dve.wait_ge(act_step, act_at("lows"))
            link(v.tensor_tensor(y2[:, 0, :], y2[:, 0, :], bn_bc[:, 0, :], ALU.add))
            link(v.tensor_tensor(y1[0:Q, 0, :], y2[0:Q, 0, :], G0[0:Q, D:2 * D], ALU.add))
            link(v.tensor_tensor(y1[Q:P, 0, :], y2[Q:P, 0, :], G1[Q:P, 0:D], ALU.add))
            link(v.scalar_tensor_tensor(y1[:, 0, :], y1[:, 0, :], 0.0, x_nat[:, 0, :], ALU.max, ALU.add))
            statistics(y1, 0)
            stage("var0")
            normalise(y1, x1, "sd0")
            stage("x1")
            dve.wait_ge(act_step, act_at("x1T"))
            link(v.tensor_tensor(flat(xT_lo), G0, flat(xT_hi).bitcast(F32), ALU.subtract))
            stage("x1T")
            lows(END["upd"] + NB, END["h1"])

            dve.wait_ge(biases_in, 80)
            for k in range(2):
                for h in range(2):
                    dve.wait_ge(act_step, act_at(f"h1_{h}"))
                    link(v.scalar_tensor_tensor(y1[:, h, :], h1[:, h, :], 1.0, bias_bc[:, k, :],
                                                ALU.mult, ALU.mult, accum_out=small[:, 12 + 2 * k + h:13 + 2 * k + h]))
                if k == 0:
                    for h in range(2):
                        link(v.tensor_scalar(y2[:, 0, h * P:(h + 1) * P], ident[:], small[:, 12 + h:13 + h], None,
                                             ALU.mult))
                    stage("al")
            dve.wait_ge(pe_step, pe_at("albc"))
            for h in range(2):
                link(v.tensor_scalar(PT[:, h, :], G0[:, 0:N], small[:, 14 + h:15 + h], None, ALU.add))
            link(v.scalar_tensor_tensor(PT[:], PT[:], SLOPE, PT[:], ALU.mult, ALU.max))
            stage("lr")
            dve.wait_ge(act_step, act_at("lrelu"))
            link(v.tensor_tensor(PT[:], PT[:], S_cnt[:, 0, :, :], ALU.mult))
            stage("ET")
            dve.wait_ge(pe_step, pe_at("hp"))
            link(v.tensor_scalar(small[:, 4:6], G0[:, 512:1024].rearrange("p (h n) -> p h n", h=2)[:, :, 0],
                                 EPS_L1, None, ALU.add))
            link(v.reciprocal(small[:, 6:8], small[:, 4:6]))
            for h in range(2):
                link(v.tensor_scalar(y1[:, h, :], G1[:, h * D:(h + 1) * D], small[:, 6 + h:7 + h], None, ALU.mult))
            link(v.tensor_scalar(y2[:], y1[:], 0.0, None, ALU.min))
            stage("hpn")
            link(v.scalar_tensor_tensor(x1[:], y1[:], 0.0, x1[:], ALU.max, ALU.add))
            dve.wait_ge(act_step, act_at("elu"))
            for h in range(2):
                link(v.scalar_tensor_tensor(y1[:, h, :], y2[:, h, :], -1.0, x1[:, h, :], ALU.add, ALU.add))
                statistics(y1, h)
            stage("var1")
            normalise(y1, y2, "sd1")
            stage("out")

        @block.tensor
        def _(pe):
            mm = nc.tensor.matmul
            said = [0]

            def stage(ins, name):
                assert PE_STAGES[said[0]] == name, name
                said[0] += 1
                ins.then_inc(pe_step, 1)

            def split_chunk(n):
                pe.wait_ge(lo_pool if by_pool(n) else lo_made, lo_count(n, by_pool(n)))
                return W_hi[:, n % NB, :], W_lo[:, n % NB, :]

            def dense(a, b, acc, hi, lo, blocks):
                for n in range(a, b):
                    W1, W0 = split_chunk(n)
                    for m in range(blocks):
                        for x_part, W_parts in ((hi, (W1, W0)), (lo, (W1,))):
                            for f in range(0, D, 512):
                                for W in W_parts:
                                    ins = mm(acc[:, m * D + f:m * D + f + 512], x_part(n - a, m), W[:, f:f + 512],
                                             start=(n == a and x_part is hi and W is W1),
                                             stop=(n == b - 1 and x_part is lo))
                    ins.then_inc(chunk_used, 1)

            def x_dense(a, b, acc):
                dense(a, b, acc, lambda c, m: xT_hi[:, c, m * P:(m + 1) * P],
                      lambda c, m: xT_lo[:, c, m * P:(m + 1) * P], 2)

            def open_bank(b):
                mm(bank(b), zero_b[0:1, 0:P], zero_b[0:1, :], start=True, stop=False, skip_group_check=True)

            pe.wait_ge(x_in, 16)
            pe.wait_ge(setup_done, 1)
            for c in range(KC):
                for h in range(2):
                    ins = nc.tensor.transpose(G0[:, c * N + h * P:c * N + (h + 1) * P], x_nat[:, h, c * P:(c + 1) * P],
                                              ident[:])
            stage(ins, "xT")
            pe.wait_ge(st_oh, 4)
            for k in range(2):
                for c in range(KC):
                    for h in range(2):
                        ins = mm(G1[:, (k * KC + c) * P:(k * KC + c + 1) * P], x_nat[:, h, c * P:(c + 1) * P],
                                 st_ohT[:, k, h, :], start=(h == 0), stop=(h == 1))
            stage(ins, "ghT")
            pe.wait_ge(dve_step, dve_at("xT"))
            mm(bank(2)[:, 0:NC], tri[:], tot[:], start=True, stop=True)
            stage(mm(bank(2)[:, NC:2 * NC], ones_b[:], tot[:], start=True, stop=True), "totals")
            pe.wait_ge(dve_step, dve_at("ghT"))
            dense(0, END["hh"], G0, lambda c, m: hh_hi[:, c // KC, c % KC, :], lambda c, m: hh_lo[:, c // KC, c % KC, :],
                  1)
            x_dense(END["hh"], END["ooA"], G1)

            def scatter_static(t):
                logits, counts = (bank(2), bank(3)) if t == 0 else (bank(0), bank(1))
                pe.wait_ge(st_made, t + 1)
                for h in range(2):
                    for r in range(3):
                        mm(logits[:, h * N:(h + 1) * N], st_scl[:, h * P:(h + 1) * P], st_scr[:, r, :],
                           start=(t <= 1 and h == 0 and r == 0), stop=(t in (0, JO) and r == 2), skip_group_check=True)
                    ins = mm(counts[:, h * N:(h + 1) * N], st_scl[:, h * P:(h + 1) * P], st_one[:],
                             start=(t <= 1 and h == 0), stop=t in (0, JO), skip_group_check=True)
                ins.then_inc(scattered, 1)

            pe.wait_ge(dve_step, dve_at("slots"))
            scatter_static(0)
            pe.wait_ge(dve_step, dve_at("D_hh"))
            x_dense(END["ooA"], END["ooB"], G0)

            def perm(s, dest):
                pe.wait_ge(placed, s + 1)

                def col(j):
                    return mm(dest[:, 0:2 * NT],
                              pos_oh[:, j, :] if isinstance(j, int) else pos_oh[:].rearrange("p j m -> p (j m)")
                              [:, bass.ds(j * P, P)],
                              tile_val[:, j, :, :].rearrange("p k t -> p (k t)") if isinstance(j, int) else
                              tile_val[:].rearrange("p j k t -> p (j k t)")[:, bass.ds(j * 2 * NT, 2 * NT)],
                              start=isinstance(j, int) and j == 0, stop=isinstance(j, int) and j == JS - 1)
                col(0)
                with pe.Fori(1, JS - 1) as j:
                    col(j)
                stage(col(JS - 1), f"perm{s}")

            pe.wait_ge(dve_step, dve_at("ooA_lo"))
            perm(0, bank(4))
            pe.wait_ge(dve_step, dve_at("ooB_lo"))
            for t in range(1, JO + 1):
                acc = G1[:, (t % 2) * D:(t % 2 + 1) * D]
                pe.wait_ge(st_oh, 4 + 4 * t)
                if t == 2:
                    pe.wait_ge(dve_step, dve_at("key0"))
                if t >= 3:
                    pe.wait_ge(reduced, t - 1)
                for i, (k, h, part) in enumerate((k, h, part) for k in range(2) for h in range(2) for part in range(2)):
                    tab = (Ao_tab, Bo_tab)[k]
                    for n in range(2):
                        ins = mm(acc[:, n * 512:(n + 1) * 512], st_ohTr[:, t % 2, k, h, :],
                                 tab[:, h, part, n * 512:(n + 1) * 512], start=(i == 0), stop=(i == 7))
                ins.then_inc(gathered, 1)
                if t >= 2:
                    scatter_static(t - 1)
            pe.wait_ge(reduced, 1 + JO)
            x_dense(END["ooB"], END["hoA"], G1)
            scatter_static(JO)
            perm(1, bank(3))
            pe.wait_ge(dve_step, dve_at("keys"))
            for k in range(2):
                ins = nc.tensor.transpose(bank(2)[0:NT, k * P:(k + 1) * P], key_col[:, k, :], ident[:])
            stage(ins, "keysT")
            pe.wait_ge(dve_step, dve_at("key_u8"))
            x_dense(END["hoA"], END["hoB"], G0)
            pe.wait_ge(dve_step, dve_at("hoB_lo"))

            open_bank(0)
            open_bank(1)

            def load(i, c):
                row = steer[0:1, i, c, :] if isinstance(i, int) else \
                    steer[0:1, bass.ds(i, 1), c, :].rearrange("p i b -> p (i b)")
                return nc.values_load_multi_w_load_instructions(
                    row, engines=(mybir.EngineType.PE,), min_val=0, max_val=(3, 3, 7)[c],
                    skip_runtime_bounds_check_because="quarters and blocks by their making")[1]

            def gather(t, b, sq, dq):
                pe.wait_ge(oh_made, t + 1)
                if not isinstance(t, int):
                    pe.wait_ge(reduced, 1 + JO + t - 1)
                elif t >= 2:
                    pe.wait_ge(reduced, 1 + JO + t - 1)
                for k, (tab, q) in enumerate(((A_tab, sq), (B_tab, dq))):
                    for n in range(2):
                        ins = mm(G1[:, (b % 2) * D + n * 512:(b % 2) * D + (n + 1) * 512], oh[:, b % 2, k, :],
                                 tab[:].rearrange("p q d -> p (q d)")[:, bass.ds(q * D + n * 512, 512)],
                                 start=(k == 0), stop=(k == 1))
                ins.then_inc(gathered, 1)

            def scatter(t, b, block64):
                pe.wait_ge(ones_made, t + 1)
                pe.wait_ge(sc_made, 2 * (t + 1))
                for r in range(2):
                    ins = mm(G0[:, bass.ds(r * 512 + block64 * Q, Q)], sc_l[:, b, :], sc_r[:, b, r, :],
                             start=False, stop=False, skip_group_check=True)
                ins.then_inc(scattered, 1)

            def ho_turn(i):
                sq, dq = load(i, 0), load(i, 1)
                late = not isinstance(i, int)
                block64 = load(i, 2) if late else None
                for b in range(U):
                    gather(U * i + b, b, sq[b], dq[b])
                    if late:
                        scatter(U * i + b - U, b, block64[b])

            ho_turn(0)
            with pe.Fori(1, TURNS) as i:
                ho_turn(i)
            block64 = load(TURNS, 2)
            for b in range(U):
                scatter(NT - U + b, b, block64[b])

            def update(a, b):
                for n in range(a, b):
                    name, k = chunks[n]
                    (hi, lo, both), c = ((xT_hi, xT_lo, x_both), (zT_hi, zT_lo, z_both))[k // KC], k % KC
                    W1, W0 = split_chunk(n)
                    first, final = k == 0, k == 2 * KC - 1
                    if n == END["hoB"] + 2:
                        pe.wait_ge(reduced, 1 + JO + NT)
                    q = 0 if name == "hn" else 1
                    acc = ps[:, (2 + 2 * q) * 512:(4 + 2 * q) * 512]
                    for f in range(0, D, 512):
                        for W in (W1, W0):
                            ins = mm(acc[:, f:f + 512], both[:, c, q, :, :].rearrange("p k n -> p (k n)"), W[:, f:f + 512], start=first and W is W1,
                                     stop=final and W is W0)
                    if q == 1:
                        for part, Ws in ((hi, (W1, W0)), (lo, (W1,))):
                            for f in range(0, D, 512):
                                for W in Ws:
                                    ins = mm(G1[:, D + f:D + f + 512], part[:, c, P:N], W[:, f:f + 512],
                                             start=first and part is hi and W is W1, stop=final and part is lo)
                    ins.then_inc(chunk_used, 1)

            pe.wait_ge(both_made, 1)
            update(END["hoB"], UX)
            pe.wait_ge(dve_step, dve_at("P"))
            for hs in range(2):
                for hd in range(2):
                    ins = nc.tensor.transpose(bank(0)[:, hs * N + hd * P:hs * N + (hd + 1) * P],
                                              S_log[:, 0, hd, hs * P:(hs + 1) * P], ident[:])
            stage(ins, "PT")
            pe.wait_ge(dve_step, dve_at("PT"))
            for s in range(2):
                if s == 1:
                    pe.wait_ge(dve_step, dve_at("zT0"))
                for c in range(4):
                    for hs in range(2):
                        d = 4 * s + c
                        ins = mm(G0[:, c * N:(c + 1) * N], x_nat[:, hs, d * P:(d + 1) * P], PT[:, hs, :],
                                 start=(hs == 0), stop=(hs == 1))
                stage(ins, f"zT{s}")
                update(UX + 2 * s, UX + 2 * s + 2)
            assert UX + 4 == END["updx"]
            pe.wait_ge(both_made, 3)
            update(END["updx"], END["upd"])
            pe.wait_ge(dve_step, dve_at("x1"))
            for c in range(KC):
                for h in range(2):
                    ins = nc.tensor.transpose(G0[:, c * N + h * P:c * N + (h + 1) * P], x1[:, h, c * P:(c + 1) * P],
                                              ident[:])
            stage(ins, "x1T")
            pe.wait_ge(dve_step, dve_at("x1T"))
            x_dense(END["upd"], END["h1"], G1)
            pe.wait_ge(dve_step, dve_at("al"))
            stage(mm(G0[:, 0:N], ones_f[:], y2[:, 0, 0:N], start=True, stop=True), "albc")
            pe.wait_ge(dve_step, dve_at("ET"))
            for hs in range(2):
                for hd in range(2):
                    mm(G0[:, 512 + hs * N:512 + hs * N + 1], PT[:, hd, hs * P:(hs + 1) * P], ones_f[:, 0:1],
                       start=(hd == 0), stop=(hd == 1))
            for hs in range(2):
                for n in range(2):
                    for hd in range(2):
                        ins = mm(G1[:, hs * D + n * 512:hs * D + (n + 1) * 512], PT[:, hd, hs * P:(hs + 1) * P],
                                 h1[:, hd, n * 512:(n + 1) * 512], start=(hd == 0), stop=(hd == 1))
            stage(ins, "hp")


_INS = ['x', 'src', 'dst', 'L0_gnn_W_hh', 'L0_gnn_b_hh', 'L0_gnn_W_oo', 'L0_gnn_b_oo', 'L0_gnn_W_ho', 'L0_gnn_b_ho',
        'L0_gnn_W_a', 'L0_gnn_b_a', 'L0_gnn_W_hn', 'L0_gnn_b_hn', 'L0_gnn_W_on', 'L0_gnn_b_on', 'L1_gnn_W', 'L1_gnn_a']


def kernel(**inputs):
    import numpy as _np
    import concourse.bacc as _bacc
    from concourse import mybir as _mybir
    from concourse.bass_utils import run_bass_kernel_spmd as _run

    nc = _bacc.Bacc("TRN2", target_bir_lowering=False, num_devices=1)
    arrays, args = {}, []
    for name in _INS:
        a = _np.ascontiguousarray(inputs[name])
        arrays[f"in_{name}_dram"] = a
        args.append(nc.dram_tensor(f"in_{name}_dram", a.shape, _mybir.dt.from_np(a.dtype), kind="ExternalInput").ap())
    args.append(nc.dram_tensor("out_0_dram", (N, D), F32, kind="ExternalOutput").ap())
    gnn_two_layers(nc, *args)
    r = _run(nc, [arrays], core_ids=[0])
    return r.results[0]["out_0_dram"]
```

```python
from contextlib import ExitStack

import concourse.bass as bass
from concourse import mybir

P = 128
N = 256
D = 1024
E = 8192
NH = 64
E_HH, E_OO = 128, 640
E_ST = E_HH + E_OO
E_HO = E - E_ST
JH = E_HO // P
JS = JH // 2
JO = E_OO // P
Q = 64
NC = (N // Q) ** 2
U = 4
NT = -(-(JH + NC - 1) // U) * U
TURNS = NT // U
LAG = 6
KC = D // P
NS = 4
NB = 4
SLOPE, EPS_L1, EPS_LN = 0.1, 1e-5, 1e-5
BIG = 3.0e38

F32 = mybir.dt.float32
F32R = mybir.dt.float32r
BF16 = mybir.dt.bfloat16
I32 = mybir.dt.int32
U8 = mybir.dt.uint8
ALU = mybir.AluOpType
ACT = mybir.ActivationFunctionType
AX = mybir.AxisListType.X


def gnn_two_layers(nc, x, src, dst, W_hh, b_hh, W_oo, b_oo, W_ho, b_ho, W_a, b_a, W_hn, b_hn, W_on, b_on,
                   L1_W, L1_a, out):
    ctx = ExitStack()
    with ctx:
        def sb(name, shape, dt=F32, stack=ctx):
            return stack.enter_context(nc.sbuf_tensor(name, shape, dt))

        def sem(name):
            return ctx.enter_context(nc.semaphore(name))

        x_nat = sb("x_nat", [P, 2, D])
        xT_hi = sb("xT_hi", [P, KC, N], F32R)
        xT_lo = sb("xT_lo", [P, KC, N], F32R)
        W_raw = sb("W_raw", [P, NS, 2, D])
        W_hi = sb("W_hi", [P, NB, D], F32R)
        W_lo = sb("W_lo", [P, NB, D], F32R)
        wa_bc = sb("wa_bc", [P, D])
        bias_bc = sb("bias_bc", [P, 2, D])
        ident = sb("ident", [P, P])
        irow = sb("irow", [P, N + 1])
        pcol = sb("pcol", [P, 4])
        tri = sb("tri", [P, P], BF16)
        ones_b = sb("ones_b", [P, P], BF16)
        ones_f = sb("ones_f", [P, P])
        zero_b = sb("zero_b", [1, 512], BF16)
        spare = sb("spare", [1, 16])
        st_col = sb("st_col", [P, 2, 1 + JO], I32)
        st_colf = sb("st_colf", [P, 2, 1 + JO])
        keys = sb("keys", [P, NT, 3])
        keys_now = sb("keys_now", [P, U, 3])
        steer = sb("steer", [1, NT + LAG, 3], I32)
        st_logit = sb("st_logit", [P, 1 + JO])
        part_f = sb("part_f", [P, 3, 1 + JO])
        part_b = sb("part_b", [P, 2, 1 + JO], BF16)
        rest = sb("rest", [P, 1 + JO])
        oh_dist = sb("oh_dist", [P, 2, 2, P], BF16)
        oh = sb("oh", [P, 2, 2, P], F32R)
        sc_l = sb("sc_l", [P, U, P])
        sc_r = sb("sc_r", [P, U, 2, Q])
        junk = sb("junk", [P, 2, D], BF16)
        small = sb("small", [P, 64])
        eps_ln = sb("eps_ln", [P, 1])
        warm = sb("warm", [P, 2])
        deviations = sb("deviations", [P, 2])
        ba_bc = sb("ba_bc", [P, 1])
        S_log = sb("S_log", [P, 3, 2, N])
        S_cnt = sb("S_cnt", [P, 3, 2, N])

        regions = ExitStack()
        A_tab = sb("A_tab", [P, 4, D], F32R, regions)
        B_tab = sb("B_tab", [P, 4, D], F32R, regions)
        Ao_tab = A_tab[:].rearrange("p (h k) d -> p h k d", h=2)
        Bo_tab = B_tab[:].rearrange("p (h k) d -> p h k d", h=2)
        hh_hi = B_tab[:, 0:2, :].rearrange("p a (c n) -> p a c n", c=KC)
        hh_lo = B_tab[:, 2:4, :].rearrange("p a (c n) -> p a c n", c=KC)
        st_row = sb("st_row", [P, 2, E_ST], I32, regions)
        st_ohT = sb("st_ohT", [P, 2, 2, P], F32, regions)
        st_ohTr = sb("st_ohTr", [P, 2, 2, 2, P], F32R, regions)
        st_scl = sb("st_scl", [P, N], BF16, regions)
        st_one = sb("st_one", [P, N], BF16, regions)
        st_scr = sb("st_scr", [P, 3, N], BF16, regions)
        sort = ExitStack()
        edges = sb("edges", [P, 2, JH], I32, sort)
        e_i = sb("e_i", [P, 2, 2, JH], I32, sort)
        cls = sb("cls", [P, JH], F32, sort)
        val = sb("val", [P, 2, JH], BF16, sort)
        tot = sb("tot", [P, NC], BF16, sort)
        cw = sb("cw", [P, 6, NC], F32, sort)
        cwi = sb("cwi", [P, 2, NC], I32, sort)
        slot = sb("slot", [P, JH], F32, sort)
        slot_i = sb("slot_i", [P, 3, JH], I32, sort)
        slot_f = sb("slot_f", [P, 2, JH], F32, sort)
        pos_oh = sb("pos_oh", [P, JS, P], BF16, sort)
        tile_oh = sb("tile_oh", [P, JS, NT], BF16, sort)
        cle = sb("cle", [P, NT, NC], BF16, sort)
        tcls = sb("tcls", [P, 2, NT], F32, sort)
        tcls_i = sb("tcls_i", [P, 5, NT], I32, sort)
        key_col = sb("key_col", [P, 2, NT], F32, sort)
        key_u8 = sb("key_u8", [NT, 2, P], U8, sort)
        ranks = ExitStack()
        cls_oh = sb("cls_oh", [P, NC, JH], F32, ranks)
        gate = sb("gate", [P, NC, JH], F32, ranks)
        cum = sb("cum", [P, NC, JH], F32, ranks)
        ranks.close()
        tile_val = sb("tile_val", [P, JS, 2, NT], BF16, sort)
        sort.close()
        key_rows = sb("key_rows", [P, 2, NT * P], U8, regions)
        x_both = sb("x_both", [P, KC, 2, 2, Q], F32R, regions)
        top_static = sb("top_static", [P, 2, N], F32, regions)
        regions.close()
        last = ExitStack()
        PT = sb("PT", [P, 2, N], F32, last)
        zT_hi = sb("zT_hi", [P, KC, N], F32R, last)
        zT_lo = sb("zT_lo", [P, KC, N], F32R, last)
        z_both = sb("z_both", [P, KC, 2, 2, Q], F32R, last)
        bn_bc = sb("bn_bc", [P, 2, D], F32, last)
        x1 = sb("x1", [P, 2, D], F32, last)
        h1 = sb("h1", [P, 2, D], F32, last)
        y1 = sb("y1", [P, 2, D], F32, last)
        y2 = sb("y2", [P, 2, D], F32, last)
        last.close()
        soft = junk[:, 0, :].bitcast(F32)

        key_dram = nc.dram_tensor("key_rows_scratch", [2, NT, P], U8, kind="Internal").ap()

        ps = ctx.enter_context(nc.psum_tensor("ps", [P, 4096], F32))
        G0, G1 = ps[:, 0:2048], ps[:, 2048:4096]

        def flat(T, a=0, b=KC):
            return T[:, a:b, :].rearrange("p c n -> p (c n)")

        def bank(b):
            return ps[:, b * 512:(b + 1) * 512]

        x_in = sem("x_in")
        edges_in = sem("edges_in")
        hh_rows_in = sem("hh_rows_in")
        st_rows_in = sem("st_rows_in")
        consts_in = sem("consts_in")
        biases_in = sem("biases_in")
        w_in = [sem(f"w_in{i}") for i in range(NS)]
        hi_made = sem("hi_made")
        lo_made = sem("lo_made")
        lo_pool = sem("lo_pool")
        chunk_used = sem("chunk_used")
        pool_done = sem("pool_done")
        dve_done = sem("dve_done")
        setup_done = sem("setup_done")
        pe_step = sem("pe_step")
        act_step = sem("act_step")
        dve_step = sem("dve_step")
        placed = sem("placed")
        keys_out = sem("keys_out")
        first_keys_back = sem("first_keys_back")
        keys_back = sem("keys_back")
        st_oh = sem("st_oh")
        st_made = sem("st_made")
        dist_made = sem("dist_made")
        oh_made = sem("oh_made")
        keys_staged = sem("keys_staged")
        gathered = sem("gathered")
        reduced = sem("reduced")
        ones_made = sem("ones_made")
        last_made = sem("last_made")
        sc_made = sem("sc_made")
        quarter_hi = sem("quarter_hi")
        scattered = sem("scattered")
        both_made = sem("both_made")
        with_x1 = sem("with_x1")
        out_in = sem("out_in")

        stream = [("hh", W_hh, k) for k in range(0, 2 * KC, 2)]
        stream += [("oo", W_oo, k) for k in range(0, 2 * KC, 2)]
        stream += [("ho", W_ho, k) for k in range(0, 2 * KC, 2)]
        for k in range(0, 2 * KC, 2):
            stream += [("hn", W_hn, k), ("on", W_on, k)]
        stream += [("l1", L1_W, k) for k in range(0, KC, 2)]
        chunks = [(name, k + i) for name, _, k in stream for i in range(2)]
        END = {"hh": 16, "ooA": 24, "ooB": 32, "hoA": 40, "hoB": 48, "updx": 64, "upd": 80, "h1": 88}

        UX = END["hoB"] + 11

        def by_pool(n):
            if n < END["hoB"] + NB:
                return n % 2 == 1 and (NB < n < END["hh"] or n >= END["ooB"] + NB)
            if n < END["hoB"] + 12:
                return True
            return n % 4 == 3

        def lo_count(n, pool):
            return sum(by_pool(m) == pool for m in range(n + 1))

        PE_STAGES = ["xT", "ghT0", "ghT1", "totals", "perm0", "perm1", "keysT", "hoB_0", "PT", "zT0", "zT1", "q1",
                     "x1T0", "x1T1", "h_0", "albc", "hp0", "hp1"]
        ACT_STAGES = ["xT", "ghT0", "ghT1", "ooA_hi", "ooB_hi0", "ooB_hi1", "soft0", "soft1", "zT0", "both0", "zT1",
                      "both1", "q0_low", "q1_low", "sd0", "x1_0", "sd1", "x1T0", "x1T1", "h1_0", "h1_1", "lrelu",
                      "relu0", "elu0", "relu1", "elu1", "sd2", "out0", "sd3"]
        DVE_STAGES = ["tot", "xT", "ghT0", "ghT1", "slots", "tiles0", "D_hh", "ooA_b", "ooA_lo", "ooB_lo", "key0",
                      "tiles1", "D_oo", "keys", "hoA_b", "hoA_lo", "key_u8", "hoB_lo", "maxima", "P", "PT", "zT0",
                      "zT1", "var0", "scale0", "var1", "x1_1", "x1T0", "x1T1", "al", "lr", "ET", "neg0", "neg1",
                      "var2", "scale2", "var3", "out1"]

        def pe_at(s):
            return PE_STAGES.index(s) + 1

        def act_at(s):
            return ACT_STAGES.index(s) + 1

        def dve_at(s):
            return DVE_STAGES.index(s) + 1

        block = ctx.enter_context(nc.Block())

        @block.sync
        def _(sp):
            for k, v in enumerate((src, dst)):
                sp.dma_start(st_row[:, k, 0:E_HH], v[0:E_HH].partition_broadcast(P)).then_inc(hh_rows_in, 16)
            sp.dma_start(x_nat[:], x.rearrange("(h p) d -> p h d", p=P)).then_inc(x_in, 16)
            for n, (name, W, k) in enumerate(stream):
                if n >= NS:
                    last_of = 2 * (n - NS) + 1
                    sp.wait_ge(lo_made, lo_count(last_of, False))
                    if lo_count(last_of, True):
                        sp.wait_ge(lo_pool, lo_count(last_of, True))
                sp.dma_start(W_raw[:, n % NS, :, :], W[k * P:(k + 2) * P, :].rearrange("(i p) d -> p i d", p=P)) \
                  .then_inc(w_in[n % NS], 16)
            sp.wait_ge(act_step, act_at("out0"))
            sp.dma_start(out[0:P, :], y2[:, 0, :]).then_inc(out_in, 16)
            sp.wait_ge(dve_step, dve_at("out1"))
            sp.dma_start(out[P:N, :], y2[:, 1, :]).then_inc(out_in, 16)
            sp.wait_ge(out_in, 32)

        @block.gpsimd
        def _(pool):
            mine = [0]

            def link(ins):
                mine[0] += 1
                ins.then_inc(pool_done, 1)
                pool.wait_ge(pool_done, mine[0])

            ga = nc.gpsimd
            exact = dict(allow_small_or_imprecise_dtypes=True)
            ga.memset(gate[:], 1.0).then_inc(pool_done, 1)
            ga.iota(irow[:], pattern=[[1, N + 1]], base=0, channel_multiplier=0, **exact).then_inc(pool_done, 1)
            ga.memset(ident[:], 0.0).then_inc(pool_done, 1)
            for h in range(2):
                ga.iota(pcol[:, 1 + h:2 + h], pattern=[[0, 1]], base=h * P, channel_multiplier=1, **exact) \
                  .then_inc(pool_done, 1)
            ga.memset(tri[:], 1.0).then_inc(pool_done, 1)
            ga.memset(ones_b[:], 1.0).then_inc(pool_done, 1)
            ga.memset(ones_f[:], 1.0).then_inc(pool_done, 1)
            ga.memset(zero_b[:], 0.0).then_inc(pool_done, 1)
            ga.memset(spare[:], 0.0).then_inc(pool_done, 1)
            ga.memset(eps_ln[:], EPS_LN).then_inc(pool_done, 1)
            pool.wait_ge(pool_done, 11)
            mine[0] = 11
            link(ga.affine_select(out=ident[:], in_=ident[:], compare_op=ALU.not_equal, fill=1.0, base=0,
                                  pattern=[[-1, P]], channel_multiplier=1))
            link(ga.affine_select(out=tri[:], in_=tri[:], compare_op=ALU.is_gt, fill=0.0, base=0,
                                  pattern=[[1, P]], channel_multiplier=-1))
            link(ga.memset(gate[:, :, 0:1], 0.0))
            for q in range(2):
                link(ga.iota(pcol[q * Q:(q + 1) * Q, 0:1], pattern=[[0, 1]], base=1, channel_multiplier=1, **exact))
            link(ga.tensor_scalar(pcol[:, 3:4], pcol[:, 0:1], -1.0, None, ALU.mult))
            ga.nop().then_inc(setup_done, 1)

            pool.wait_ge(hh_rows_in, 32)
            for k in range(2):
                for h in range(2):
                    ga.tensor_scalar(st_ohT[:, k, h, :], st_row[:, k, 0:P], pcol[:, 1 + h:2 + h], None,
                                     ALU.is_equal).then_inc(st_oh, 1)

            def oo_onehots(t):
                if t >= 3:
                    pool.wait_ge(gathered, t - 2)
                for k in range(2):
                    edges_of = st_row[:, k, E_HH:E_ST].rearrange("p (m t) -> p t m", t=JO)[:, t - 1, :]
                    for h in range(2):
                        ga.tensor_scalar(st_ohTr[:, t % 2, k, h, :], edges_of, pcol[:, 1 + h:2 + h], None,
                                         ALU.is_equal).then_inc(st_oh, 1)

            def place(s):
                cols = slice(s * JS, (s + 1) * JS)
                if s == 0:
                    pool.wait_ge(dve_step, dve_at("slots"))
                    link(ga.tensor_tensor(pos_oh[:], slot_f[:, 1, cols].unsqueeze(2).broadcast_to([P, JS, P]),
                                          irow[:, 0:P].unsqueeze(1).broadcast_to([P, JS, P]), ALU.subtract))
                    link(ga.tensor_scalar(pos_oh[:], pos_oh[:], 0.0, None, ALU.is_equal))
                pool.wait_ge(dve_step, dve_at(f"tiles{s}"))
                for k in range(2):
                    ins = ga.tensor_tensor(tile_val[:, :, k, :], tile_oh[:],
                                           val[:, k, cols].unsqueeze(2).broadcast_to([P, JS, NT]), ALU.mult)
                    link(ins)
                ga.nop().then_inc(placed, 1)

            def lows(a, b):
                for n in range(a, b):
                    if by_pool(n):
                        pool.wait_ge(hi_made, n + 1)
                        ga.tensor_tensor(W_lo[:, n % NB, :], W_raw[:, n // 2 % NS, n % 2, :],
                                         W_hi[:, n % NB, :].bitcast(F32), ALU.subtract).then_inc(lo_pool, 1)

            pool.wait_ge(st_rows_in, 32)
            oo_onehots(1)
            oo_onehots(2)
            lows(0, END["hh"])
            place(0)
            oo_onehots(3)
            oo_onehots(4)
            oo_onehots(5)
            place(1)

            def settle(n):
                ga.tensor_tensor(spare[0:1, n:n + 1], zero_b[0:1, 0:1], zero_b[0:1, 1:2], ALU.add)

            def ho_turn(i):
                first = isinstance(i, int)
                if not first:
                    pool.wait_ge(sc_made, 2 * U * i)
                pool.wait_ge(reduced, 1 + JO + U * (i + 1))
                if not first:
                    settle(0)
                ga.tensor_copy(keys_now[:], keys[:, 0:U, :] if first else keys[:, bass.ds(U * i, U), :]) \
                    .then_inc(keys_staged, 1)
                pool.wait_ge(keys_staged, i + 1)
                for b in range(U):
                    if not first and b % 2 == 0:
                        pool.wait_ge(scattered, 1 + JO + U * (i - 1) + b + 2)
                        settle(1 + b)
                    ga.tensor_scalar(sc_r[:, b, 0, :], irow[:, 1:Q + 1], keys_now[:, b, 0:1],
                                     keys_now[:, b, 2:3], ALU.is_equal, ALU.mult).then_inc(sc_made, 1)
                    ga.tensor_scalar(sc_l[:, b, :], irow[:, 1:P + 1], keys_now[:, b, 1:2], None,
                                     ALU.is_equal).then_inc(sc_made, 1)

            lows(END["hh"], END["hoA"] + NB + 2)
            pool.wait_ge(dve_step, dve_at("key_u8"))
            pool.dma_start(key_dram.rearrange("k t m -> t k m"), key_u8[:]).then_inc(keys_out, 16)
            lows(END["hoA"] + NB + 2, END["hoA"] + NB + 4)
            pool.wait_ge(keys_out, 16)
            for a, b in ((0, 2), (2, NT)):
                pool.dma_start(key_rows[:, :, a * P:b * P],
                               key_dram[:, a:b, :].rearrange("k t m -> k (t m)").partition_broadcast(P)) \
                                   .then_inc(keys_back if a else first_keys_back, 16)
            for q in range(2):
                for i, part in enumerate((xT_hi, xT_lo) if q == 0 else (xT_lo, xT_hi)):
                    ga.tensor_copy(x_both[:, :, q, i, :], part[:, :, q * Q:(q + 1) * Q]).then_inc(both_made, 1)
            lows(END["hoA"] + NB + 4, END["hoB"] + NB)
            ho_turn(0)
            with pool.Fori(1, TURNS - 1) as i:
                ho_turn(i)

            lows(END["hoB"] + NB, len(chunks))
            for h in range(2):
                pool.wait_ge(act_step, act_at(f"relu{h}"))
                ga.tensor_tensor(y1[:, h, :], y1[:, h, :], x1[:, h, :], ALU.add).then_inc(with_x1, 1)

        @block.scalar
        def _(act):
            sa = nc.scalar
            for k, v in enumerate((src, dst)):
                act.dma_start(edges[:, k, :], v[E_ST:E].rearrange("(p j) -> p j", p=P)).then_inc(edges_in, 16)
            for k, v in enumerate((src, dst)):
                act.dma_start(st_row[:, k, E_HH:], v[E_HH:E_ST].partition_broadcast(P)).then_inc(st_rows_in, 16)
            for k, v in enumerate((src, dst)):
                act.dma_start(st_col[:, k, 0:1], v[0:E_HH].rearrange("(p j) -> p j", p=P)).then_inc(consts_in, 16)
                act.dma_start(st_col[:, k, 1:], v[E_HH:E_ST].rearrange("(p j) -> p j", p=P)).then_inc(consts_in, 16)
            act.dma_start(wa_bc[:], W_a.rearrange("d o -> (d o)").partition_broadcast(P)).then_inc(consts_in, 16)
            act.dma_start(ba_bc[:], b_a.partition_broadcast(P)).then_inc(consts_in, 16)
            act.dma_start(bias_bc[:, 0, :], b_hh.partition_broadcast(P)).then_inc(biases_in, 16)
            act.dma_start(bias_bc[:, 1, :], b_oo.partition_broadcast(P)).then_inc(biases_in, 16)

            def high(n):
                act.wait_ge(w_in[n // 2 % NS], 16 * (n // 2 // NS + 1))
                if n >= NB:
                    act.wait_ge(chunk_used, n - NB + 1)
                sa.copy(W_hi[:, n % NB, :], W_raw[:, n // 2 % NS, n % 2, :]).then_inc(hi_made, 1)

            def highs(a, b):
                for n in range(a + NB, min(b + NB, len(chunks))):
                    high(n)

            act.wait_ge(pe_step, pe_at("xT"))
            sa.copy(flat(xT_hi), G0).then_inc(act_step, 1)
            for k in range(2):
                for n in range(k * NB // 2, (k + 1) * NB // 2):
                    high(n)
                act.wait_ge(pe_step, pe_at(f"ghT{k}"))
                sa.copy(hh_hi[:, k, :, :].rearrange("p c n -> p (c n)"), G1[:, k * D:(k + 1) * D]).then_inc(act_step, 1)
            highs(0, END["ooA"])
            act.wait_ge(dve_step, dve_at("ooA_b"))
            sa.copy(Ao_tab[:, :, 0, :], G1.rearrange("p (h d) -> p h d", h=2)).then_inc(act_step, 1)
            highs(END["ooA"], END["ooB"] - 1)
            act.wait_ge(chunk_used, END["ooB"])
            for h in range(2):
                sa.copy(Bo_tab[:, h, 0, :], G0[:, h * D:(h + 1) * D]).then_inc(act_step, 1)
            act.wait_ge(dve_step, dve_at("D_hh"))
            act.dma_start(bias_bc[:, 0, :], b_ho.partition_broadcast(P)).then_inc(biases_in, 16)
            highs(END["ooB"] - 1, END["hoA"])

            def table_high(tab, acc, a, b):
                for q in range(a, b):
                    r = (q % 2) * Q
                    sa.copy(tab[0:Q, q, :], acc[r:r + Q, (q // 2) * D:(q // 2 + 1) * D]).then_inc(quarter_hi, 1)

            act.wait_ge(dve_step, dve_at("hoA_b"))
            table_high(A_tab, G1, 0, 4)
            for k in range(2):
                act.dma_start(bias_bc[:, k, :], L1_a[0, k * D:(k + 1) * D].partition_broadcast(P)) \
                   .then_inc(biases_in, 16)
            highs(END["hoA"], END["hoA"] + NB)
            act.wait_ge(pe_step, pe_at("hoB_0"))
            table_high(B_tab, G0, 0, 2)
            highs(END["hoA"] + NB, END["hoB"] - 1)
            act.wait_ge(chunk_used, END["hoB"])
            table_high(B_tab, G0, 2, 4)

            def distance(t, b):
                k = key_rows[:, :, t * P:(t + 1) * P] if isinstance(t, int) else key_rows[:, :, bass.ds(t * P, P)]
                sa.activation(oh_dist[:, b, :, :], k, ACT.Abs, bias=pcol[:, 3:4]).then_inc(dist_made, 1)

            def onehot(t, b):
                act.wait_ge(dist_made, t + 1)
                if not isinstance(t, int) or t >= 1:
                    act.wait_ge(oh_made, t)
                    act.wait_ge(gathered, JO + t - 1)
                sa.activation(oh[:, b, :, :], oh_dist[:, b, :, :], ACT.Relu, bias=1.0, scale=-1.0) \
                  .then_inc(oh_made, 1)

            act.wait_ge(first_keys_back, 16)
            distance(0, 0)
            onehot(0, 0)
            distance(1, 1)
            high(END["hoB"] + NB - 1)
            act.wait_ge(keys_back, 16)
            with act.Fori(1, NT // 2) as i:
                onehot(2 * i - 1, 1)
                distance(2 * i, 0)
                onehot(2 * i, 0)
                distance(2 * i + 1, 1)
            onehot(NT - 1, 1)

            act.wait_ge(gathered, JO + NT)
            act.dma_start(bn_bc[0:Q, 0, :], b_hn.partition_broadcast(Q)).then_inc(biases_in, 16)
            act.dma_start(bn_bc[Q:P, 0, :], b_on.partition_broadcast(Q)).then_inc(biases_in, 16)
            act.dma_start(bn_bc[:, 1, :], b_on.partition_broadcast(P)).then_inc(biases_in, 16)
            highs(END["hoB"], END["hoB"] + 6)
            act.wait_ge(dve_step, dve_at("maxima"))
            for h in range(2):
                sa.activation(S_log[:, :, h, :], S_log[:, :, h, :], ACT.Exp, bias=small[:, h:h + 1]) \
                    .then_inc(act_step, 1)
            highs(END["hoB"] + 6, UX)
            for s in range(2):
                act.wait_ge(pe_step, pe_at(f"zT{s}"))
                sa.copy(flat(zT_hi, 4 * s, 4 * s + 4), G0[:, 0:D]).then_inc(act_step, 1)
                act.wait_ge(act_step, act_at(f"zT{s}"))
                for q in range(2):
                    ins = sa.copy(z_both[:, 4 * s:4 * s + 4, q, q, :],
                                  zT_hi[:, 4 * s:4 * s + 4, q * Q:(q + 1) * Q])
                ins.then_inc(act_step, 1)
                highs(UX + 2 * s, UX + 2 * s + 2)
            highs(UX + 4, END["upd"] - 2)
            def deviation(h):
                sa.activation(deviations[:, h:h + 1], small[:, 41 + 2 * h:42 + 2 * h], ACT.Sqrt, bias=eps_ln[:, 0:1]) \
                    .then_inc(act_step, 1)

            def warm_up(func, to):
                sa.activation(warm[:, to:to + 1], eps_ln[:, 0:1], func)

            warm_up(ACT.Sqrt, 0)
            act.wait_ge(chunk_used, END["upd"] - 2)
            sa.copy(y2[0:Q, 0, :], G0[Q:P, D:2 * D]).then_inc(act_step, 1)
            act.wait_ge(pe_step, pe_at("q1"))
            sa.copy(y2[Q:P, 0, :], G1[0:Q, 0:D]).then_inc(act_step, 1)
            highs(END["upd"] - 2, END["upd"])

            def normalise_first_half(dest):
                sa.activation(dest, y1[:, 0, :], ACT.Identity, bias=small[:, 10:11], scale=small[:, 8:9]) \
                    .then_inc(act_step, 1)

            act.wait_ge(dve_step, dve_at("var0"))
            deviation(0)
            act.wait_ge(dve_step, dve_at("scale0"))
            normalise_first_half(x1[:, 0, :])
            act.wait_ge(dve_step, dve_at("var1"))
            deviation(1)
            for h in range(2):
                act.wait_ge(pe_step, pe_at(f"x1T{h}"))
                sa.copy(xT_hi[:, :, h * P:(h + 1) * P], G0[:, h * D:(h + 1) * D].rearrange("p (c n) -> p c n", n=P)) \
                    .then_inc(act_step, 1)
            highs(END["upd"], END["h1"])
            warm_up(ACT.Exp, 1)
            act.wait_ge(pe_step, pe_at("h_0"))
            sa.copy(h1[:, 0, :], G1[:, 0:D]).then_inc(act_step, 1)
            act.wait_ge(chunk_used, END["h1"])
            sa.copy(h1[:, 1, :], G1[:, D:2 * D]).then_inc(act_step, 1)
            act.wait_ge(dve_step, dve_at("lr"))
            sa.activation(PT[:], PT[:], ACT.Exp, scale=-1.0).then_inc(act_step, 1)
            for h in range(2):
                act.wait_ge(dve_step, dve_at(f"neg{h}"))
                sa.activation(y1[:, h, :], G1[:, h * D:(h + 1) * D], ACT.Relu, scale=small[:, 6 + h:7 + h]) \
                    .then_inc(act_step, 1)
                sa.activation(y2[:, h, :], y2[:, h, :], ACT.Exp).then_inc(act_step, 1)
            warm_up(ACT.Sqrt, 0)
            act.wait_ge(dve_step, dve_at("var2"))
            deviation(0)
            act.wait_ge(dve_step, dve_at("scale2"))
            normalise_first_half(y2[:, 0, :])
            act.wait_ge(dve_step, dve_at("var3"))
            deviation(1)

        @block.vector
        def _(dve):
            v = nc.vector
            mine = [0]

            def link(ins):
                mine[0] += 1
                ins.then_inc(dve_done, 1)
                dve.wait_ge(dve_done, mine[0])

            said = [0]

            def stage(name):
                assert DVE_STAGES[said[0]] == name, name
                said[0] += 1
                v.nop().then_inc(dve_step, 1)

            def low(n):
                if not by_pool(n):
                    dve.wait_ge(hi_made, n + 1)
                    v.tensor_tensor(W_lo[:, n % NB, :], W_raw[:, n // 2 % NS, n % 2, :],
                                    W_hi[:, n % NB, :].bitcast(F32), ALU.subtract).then_inc(lo_made, 1)

            def lows(a, b):
                for n in range(a, b):
                    low(n)

            dve.wait_ge(edges_in, 32)
            link(v.tensor_scalar(e_i[:, 0, :, :], edges[:], 6, None, ALU.logical_shift_right))
            link(v.tensor_scalar(e_i[:, 1, :, :], edges[:], Q - 1, None, ALU.bitwise_and))
            link(v.scalar_tensor_tensor(cls[:], e_i[:, 0, 0, :], 4.0, e_i[:, 0, 1, :], ALU.mult, ALU.add))
            link(v.tensor_scalar(val[:], e_i[:, 1, :, :], 1.0, None, ALU.add))
            dve.wait_ge(setup_done, 1)
            link(v.tensor_tensor(cls_oh[:], cls[:].unsqueeze(1).broadcast_to([P, NC, JH]),
                                 irow[:, 0:NC].unsqueeze(2).broadcast_to([P, NC, JH]), ALU.is_equal))
            link(v.tensor_tensor_scan(cum[:].rearrange("p c j -> p (c j)"), gate[:].rearrange("p c j -> p (c j)"),
                                      cls_oh[:].rearrange("p c j -> p (c j)"), 0.0, ALU.mult, ALU.add))
            link(v.tensor_copy(tot[:], cum[:, :, JH - 1]))
            stage("tot")
            dve.wait_ge(act_step, act_at("xT"))
            link(v.tensor_tensor(flat(xT_lo), G0, flat(xT_hi).bitcast(F32), ALU.subtract))
            stage("xT")
            for k in range(2):
                lows(k * NB // 2, (k + 1) * NB // 2)
                dve.wait_ge(act_step, act_at(f"ghT{k}"))
                link(v.tensor_tensor(hh_lo[:, k, :, :].rearrange("p c n -> p (c n)"), G1[:, k * D:(k + 1) * D],
                                     hh_hi[:, k, :, :].rearrange("p c n -> p (c n)").bitcast(F32), ALU.subtract))
                stage(f"ghT{k}")

            low(NB)
            dve.wait_ge(pe_step, pe_at("totals"))
            pre, allc = bank(2)[:, 0:NC], bank(2)[:, NC:2 * NC]
            link(v.tensor_scalar(cwi[:, 0, :], allc, float(P - 1), None, ALU.add))
            link(v.tensor_scalar(cwi[:, 1, :], cwi[:, 0, :], 7, None, ALU.logical_shift_right))
            link(v.tensor_copy(cw[:, 0, :], cwi[:, 1, :]))
            link(v.memset(cw[:, 5, :], 1.0))
            link(v.tensor_tensor_scan(cw[:, 1, :], cw[:, 5, :], cw[:, 0, :], 0.0, ALU.mult, ALU.add))
            link(v.tensor_tensor(cw[:, 2, :], cw[:, 1, :], cw[:, 0, :], ALU.subtract))
            link(v.tensor_scalar(cw[:, 3, :], cw[:, 2, :], float(P), -1.0, ALU.mult, ALU.add))
            link(v.tensor_tensor(cw[:, 4, :], cw[:, 3, :], pre, ALU.add))
            low(NB + 1)
            link(v.tensor_tensor(cum[:], cum[:], cw[:, 4, :].unsqueeze(2).broadcast_to([P, NC, JH]), ALU.add))
            link(v.tensor_tensor(cum[:], cum[:], cls_oh[:], ALU.mult))
            low(NB + 2)
            link(v.tensor_reduce(slot[:], cum[:].rearrange("p c j -> p j c"), AX, ALU.add))
            low(NB + 3)
            link(v.tensor_copy(slot_i[:, 0, :], slot[:]))
            link(v.tensor_scalar(slot_i[:, 1, :], slot_i[:, 0, :], 7, None, ALU.logical_shift_right))
            link(v.tensor_scalar(slot_i[:, 2, :], slot_i[:, 0, :], P - 1, None, ALU.bitwise_and))
            link(v.tensor_copy(slot_f[:], slot_i[:, 1:3, :]))
            stage("slots")
            lows(NB + 4, END["hh"] + NB)

            def tiles(s):
                link(v.tensor_tensor(tile_oh[:], slot_f[:, 0, s * JS:(s + 1) * JS].unsqueeze(2)
                                     .broadcast_to([P, JS, NT]), irow[:, 0:NT].unsqueeze(1)
                                     .broadcast_to([P, JS, NT]), ALU.is_equal))
                stage(f"tiles{s}")

            def places(s):
                link(v.tensor_tensor(pos_oh[:], slot_f[:, 1, s * JS:(s + 1) * JS].unsqueeze(2)
                                     .broadcast_to([P, JS, P]), irow[:, 0:P].unsqueeze(1)
                                     .broadcast_to([P, JS, P]), ALU.is_equal))

            def static_logit(t):
                if t == 0:
                    acc = G0[:, 0:D]
                    dve.wait_ge(chunk_used, END["hh"])
                    dve.wait_ge(biases_in, 32)
                    dve.wait_ge(consts_in, 96)
                    link(v.tensor_copy(st_colf[:], st_col[:]))
                    link(v.tensor_tensor(acc, acc, bias_bc[:, 0, :], ALU.add))
                else:
                    acc = G1[:, (t % 2) * D:(t % 2 + 1) * D]
                    dve.wait_ge(gathered, t)
                link(v.scalar_tensor_tensor(junk[:, 0, :], acc, 0.0, wa_bc[:], ALU.max, ALU.mult,
                                            accum_out=st_logit[:, t:t + 1]))
                v.nop().then_inc(reduced, 1)

            def split_logits(a, b):
                link(v.tensor_copy(part_b[:, 0, a:b], st_logit[:, a:b]))
                link(v.tensor_copy(part_f[:, 0, a:b], part_b[:, 0, a:b]))
                link(v.tensor_tensor(rest[:, a:b], st_logit[:, a:b], part_f[:, 0, a:b], ALU.subtract))
                link(v.tensor_copy(part_b[:, 1, a:b], rest[:, a:b]))
                link(v.tensor_copy(part_f[:, 1, a:b], part_b[:, 1, a:b]))
                link(v.tensor_tensor(part_f[:, 2, a:b], rest[:, a:b], part_f[:, 1, a:b], ALU.subtract))

            def static_operands(t):
                if t >= 1:
                    dve.wait_ge(scattered, t)
                v.tensor_scalar(st_scl[:], irow[:, 0:N], st_colf[:, 1, t:t + 1], None, ALU.is_equal)
                v.tensor_scalar(st_one[:], irow[:, 0:N], st_colf[:, 0, t:t + 1], None, ALU.is_equal)
                for r in range(3):
                    ins = v.tensor_scalar(st_scr[:, r, :], irow[:, 0:N], st_colf[:, 0, t:t + 1],
                                          part_f[:, r, t:t + 1], ALU.is_equal, ALU.mult)
                link(ins)
                v.nop().then_inc(st_made, 1)

            def take_sums(kind, logits, counts):
                C, L = (T[:, kind, :, :].rearrange("p h (q n) -> p (h q) n", q=counts.shape[1] // 2)
                        for T in (S_cnt, S_log))
                link(v.tensor_copy(C, counts))
                link(v.tensor_copy(L, logits))

            def mean_logits(kind):
                Cf, Lf = (T[:, kind, :, :].rearrange("p h n -> p (h n)") for T in (S_cnt, S_log))
                link(v.tensor_scalar(soft, Cf, 1.0, None, ALU.max))
                link(v.reciprocal(soft, soft))
                link(v.tensor_tensor(Lf, Lf, soft, ALU.mult))
                link(v.tensor_scalar(soft, Cf, 0.0, -BIG, ALU.is_equal, ALU.mult))
                link(v.scalar_tensor_tensor(Lf, Lf, ba_bc[:, 0:1], soft, ALU.add, ALU.add))

            static_logit(0)
            low(END["hh"] + NB)
            split_logits(0, 1)
            static_operands(0)
            low(END["hh"] + NB + 1)
            tiles(0)
            lows(END["hh"] + NB + 2, END["hh"] + NB + 4)
            lows(END["hh"] + NB + 4, END["hh"] + NB + 6)
            dve.wait_ge(scattered, 1)
            take_sums(0, *(bank(b).rearrange("p (h n) -> p h n", h=2) for b in (2, 3)))
            stage("D_hh")
            lows(END["hh"] + NB + 6, END["ooA"] + NB)

            def add_bias(acc, k):
                for h in range(2):
                    link(v.tensor_tensor(acc[:, h * D:(h + 1) * D], acc[:, h * D:(h + 1) * D], bias_bc[:, k, :],
                                         ALU.add))

            def low_half(tab, acc, h):
                link(v.tensor_tensor(tab[:, h, 1, :], acc[:, h * D:(h + 1) * D],
                                     tab[:, h, 0, :].bitcast(F32), ALU.subtract))

            def low_quarter(tab, acc, before, a, b):
                for q in range(a, b):
                    r = (q % 2) * Q
                    dve.wait_ge(quarter_hi, before + q + 1)
                    link(v.tensor_tensor(tab[Q:P, q, :], acc[r:r + Q, (q // 2) * D:(q // 2 + 1) * D],
                                         tab[0:Q, q, :].bitcast(F32), ALU.subtract))

            dve.wait_ge(chunk_used, END["ooA"])
            add_bias(G1, 1)
            stage("ooA_b")
            dve.wait_ge(act_step, act_at("ooA_hi"))
            for h in range(2):
                low_half(Ao_tab, G1, h)
            stage("ooA_lo")
            lows(END["ooA"] + NB, END["ooB"] + NB - 1)
            for h in range(2):
                dve.wait_ge(act_step, act_at(f"ooB_hi{h}"))
                low_half(Bo_tab, G0, h)
            stage("ooB_lo")
            low(END["ooB"] + NB - 1)
            dve.wait_ge(pe_step, pe_at("perm0"))
            link(v.tensor_copy(key_col[:].rearrange("p k t -> p (k t)"), bank(4)[:, 0:2 * NT]))
            stage("key0")
            places(1)
            static_logit(1)
            tiles(1)
            static_logit(2)
            link(v.tensor_tensor(cle[:], cw[:, 1, :].unsqueeze(1).broadcast_to([P, NT, NC]),
                                 irow[:, 0:NT].unsqueeze(2).broadcast_to([P, NT, NC]), ALU.is_le))
            static_logit(3)
            link(v.tensor_reduce(tcls[:, 0, :], cle[:], AX, ALU.add))
            link(v.tensor_scalar(tcls_i[:, 0, :], tcls[:, 0, :], float(NC - 1), None, ALU.min))
            link(v.tensor_scalar(tcls_i[:, 1, :], tcls_i[:, 0, :], 2, None, ALU.logical_shift_right))
            link(v.tensor_scalar(tcls_i[:, 2, :], tcls_i[:, 0, :], 3, None, ALU.bitwise_and))
            static_logit(4)
            link(v.tensor_scalar(tcls_i[:, 3, :], tcls_i[:, 2, :], 1, None, ALU.bitwise_and))
            link(v.tensor_scalar(tcls_i[:, 4, :], tcls_i[:, 2, :], 1, None, ALU.logical_shift_right))
            link(v.scalar_tensor_tensor(tcls_i[:, 0, :], tcls_i[:, 4, :], 4.0, tcls_i[:, 1, :], ALU.mult, ALU.add))
            static_logit(5)
            assert JO == 5
            link(v.memset(steer[:], 0))
            for c in range(2):
                link(v.tensor_scalar(steer[0:1, 0:NT, c], tcls_i[0:1, 1 + c, :], float(D), None, ALU.mult))
            link(v.tensor_scalar(steer[0:1, LAG:, 2], tcls_i[0:1, 0, :], float(2 * Q), None, ALU.mult))
            link(v.tensor_scalar(tcls[:, 1, :], tcls_i[:, 3, :], float(Q), None, ALU.mult))
            split_logits(1, 1 + JO)
            static_operands(1)
            low(END["ooB"] + NB)
            mean_logits(0)
            for t in range(2, 1 + JO):
                low(END["ooB"] + NB + t - 1)
                static_operands(t)
            lows(END["ooB"] + NB + JO, END["hoA"] + NB - 1)
            dve.wait_ge(scattered, 1 + JO)
            take_sums(1, *(bank(b).rearrange("p (h n) -> p h n", h=2) for b in (0, 1)))
            stage("D_oo")
            low(END["hoA"] + NB - 1)
            dve.wait_ge(pe_step, pe_at("perm1"))
            link(v.tensor_tensor(key_col[:].rearrange("p k t -> p (k t)"), key_col[:].rearrange("p k t -> p (k t)"),
                                 bank(3)[:, 0:2 * NT], ALU.add))
            link(v.tensor_copy(keys[:, :, 0], key_col[:, 0, :]))
            link(v.tensor_tensor(keys[:, :, 1], key_col[:, 1, :], tcls[:, 1, :], ALU.add))
            stage("keys")
            dve.wait_ge(biases_in, 48)
            dve.wait_ge(chunk_used, END["hoA"])
            add_bias(G1, 0)
            stage("hoA_b")
            low_quarter(A_tab, G1, 0, 0, 4)
            stage("hoA_lo")
            low(END["hoA"] + NB)
            dve.wait_ge(pe_step, pe_at("keysT"))
            link(v.tensor_copy(key_u8[:].rearrange("t k m -> t (k m)"), bank(4)[0:NT, 0:2 * P]))
            stage("key_u8")
            lows(END["hoA"] + NB + 1, END["hoA"] + NB + 4)
            mean_logits(1)
            link(v.tensor_tensor(top_static[:], S_log[:, 0, :, :], S_log[:, 1, :, :], ALU.max))
            low_quarter(B_tab, G0, 4, 0, 2)
            lows(END["hoA"] + NB + 4, END["hoB"] + NB - 1)
            low_quarter(B_tab, G0, 4, 2, 4)
            stage("hoB_lo")

            def reduce_tile(t, b):
                acc = G1[:, (b % 2) * D:(b % 2 + 1) * D]
                dve.wait_ge(gathered, JO + 1 + t)
                v.scalar_tensor_tensor(junk[:, b % 2, :], acc, 0.0, wa_bc[:], ALU.max, ALU.mult,
                                       accum_out=keys[:, t:t + 1, 2] if isinstance(t, int) else
                                       keys[:, bass.ds(t, 1), 2]).then_inc(reduced, 1)

            def ones_tile(t, b, peeled):
                if not peeled or t >= U:
                    dve.wait_ge(scattered, 1 + JO + t - U + 1)
                v.tensor_scalar(sc_r[:, b, 1, :], irow[:, 1:Q + 1], keys[:, t:t + 1, 0] if peeled else
                                keys[:, bass.ds(t, 1), 0], None, ALU.is_equal).then_inc(ones_made, 1)

            for t in range(2 * U):
                reduce_tile(t, t % U)
                if t >= U:
                    ones_tile(t - U, t % U, True)
            low(END["hoB"] + NB - 1)
            with dve.Fori(2, TURNS) as i:
                for b in range(U):
                    reduce_tile(U * i + b, b)
                    ones_tile(U * i + b - U, b, False)
            dve.wait_ge(reduced, 1 + JO + NT)
            for t in range(NT - U, NT):
                ones_tile(t, t % U, True)
                v.tensor_scalar(sc_r[:, t % U, 0, :], irow[:, 1:Q + 1], keys[:, t, 0:1], keys[:, t, 2:3],
                                ALU.is_equal, ALU.mult)
                v.tensor_scalar(sc_l[:, t % U, :], irow[:, 1:P + 1], keys[:, t, 1:2], None,
                                ALU.is_equal).then_inc(last_made, 1)
            dve.wait_ge(reduced, 1 + JO + NT)

            dve.wait_ge(scattered, 1 + JO + NT)
            take_sums(2, *(G0[:, 0:D].rearrange("p (g r n) -> p r g n", r=2, n=Q)[:, r, :, :] for r in range(2)))
            mean_logits(2)
            link(v.tensor_tensor(top_static[:], top_static[:], S_log[:, 2, :, :], ALU.max))
            link(v.tensor_reduce(small[:, 2:4], top_static[:], AX, ALU.max))
            link(v.tensor_scalar(small[:, 0:2], small[:, 2:4], -1.0, None, ALU.mult))
            stage("maxima")
            for h in range(2):
                dve.wait_ge(act_step, act_at(f"soft{h}"))
                link(v.tensor_tensor(S_log[:, :, h, :], S_log[:, :, h, :], S_cnt[:, :, h, :], ALU.mult))
                for kind in range(1, 3):
                    link(v.tensor_tensor(S_log[:, 0, h, :], S_log[:, 0, h, :], S_log[:, kind, h, :], ALU.add))
            link(v.tensor_reduce(small[:, 4:6], S_log[:, 0, :, :], AX, ALU.add))
            link(v.tensor_scalar(small[:, 6:8], small[:, 4:6], 0.0, None, ALU.is_equal))
            link(v.tensor_tensor(small[:, 4:6], small[:, 4:6], small[:, 6:8], ALU.add))
            link(v.reciprocal(small[:, 6:8], small[:, 4:6]))
            for h in range(2):
                link(v.tensor_scalar(S_log[:, 0, h, :], S_log[:, 0, h, :], small[:, 6 + h:7 + h], None, ALU.mult))
            stage("P")
            dve.wait_ge(pe_step, pe_at("PT"))
            link(v.tensor_copy(PT[:].rearrange("p h n -> p (h n)"), bank(0)))
            stage("PT")
            lows(UX, UX + NB)
            for s in range(2):
                dve.wait_ge(act_step, act_at(f"zT{s}"))
                own = (4 * s, 4 * s + 4)
                link(v.tensor_tensor(flat(zT_lo, *own), G0[:, 0:D], flat(zT_hi, *own).bitcast(F32), ALU.subtract))
                for q in range(2):
                    of = (slice(None), slice(*own), slice(q * Q, (q + 1) * Q))
                    link(v.tensor_copy(z_both[:, slice(*own), q, 1 - q, :], zT_lo[of]))
                dve.wait_ge(act_step, act_at(f"both{s}"))
                stage(f"zT{s}")
                lows(UX + NB + 2 * s, UX + NB + 2 * s + 2)
            lows(UX + NB + 4, END["upd"] + NB - 2)
            link(v.tensor_tensor(S_cnt[:, 0, :, :], S_cnt[:, 0, :, :], S_cnt[:, 1, :, :], ALU.add))
            link(v.tensor_tensor(S_cnt[:, 0, :, :], S_cnt[:, 0, :, :], S_cnt[:, 2, :, :], ALU.add))

            def statistics(h):
                for g in range(2):
                    link(v.bn_stats(small[:, 16 + 12 * h + 6 * g:22 + 12 * h + 6 * g], y1[:, h, g * 512:(g + 1) * 512]))
                link(v.bn_aggr(small[:, 40 + 2 * h:42 + 2 * h], small[:, 16 + 12 * h:28 + 12 * h]))

            def first_half_scale(deviation):
                dve.wait_ge(act_step, act_at(deviation))
                link(v.reciprocal(small[:, 8:9], deviations[:, 0:1]))
                link(v.tensor_scalar(small[:, 10:11], small[:, 40:41], small[:, 8:9], -1.0, ALU.mult, ALU.mult))

            def normalise_second_half(dest, deviation):
                dve.wait_ge(act_step, act_at(deviation))
                link(v.reciprocal(small[:, 9:10], deviations[:, 1:2]))
                link(v.tensor_scalar(dest, y1[:, 1, :], small[:, 42:43], small[:, 9:10], ALU.subtract, ALU.mult))

            dve.wait_ge(biases_in, 128)
            for q, acc in ((0, G0[:, D:2 * D]), (1, G1[:, 0:D])):
                own = slice(q * Q, (q + 1) * Q)
                dve.wait_ge(act_step, act_at(f"q{q}_low"))
                link(v.tensor_tensor(y2[own, 0, :], y2[own, 0, :], bn_bc[own, 0, :], ALU.add))
                link(v.tensor_tensor(y1[own, 0, :], y2[own, 0, :], acc[own, :], ALU.add))
            link(v.scalar_tensor_tensor(y1[:, 0, :], y1[:, 0, :], 0.0, x_nat[:, 0, :], ALU.max, ALU.add))
            statistics(0)
            stage("var0")
            dve.wait_ge(chunk_used, END["upd"])
            link(v.tensor_tensor(y1[:, 1, :], G1[:, D:2 * D], bn_bc[:, 1, :], ALU.add))
            first_half_scale("sd0")
            stage("scale0")
            link(v.scalar_tensor_tensor(y1[:, 1, :], y1[:, 1, :], 0.0, x_nat[:, 1, :], ALU.max, ALU.add))
            statistics(1)
            stage("var1")
            normalise_second_half(x1[:, 1, :], "sd1")
            stage("x1_1")
            lows(END["upd"] + NB - 2, END["upd"] + NB)
            for h in range(2):
                dve.wait_ge(act_step, act_at(f"x1T{h}"))
                own = slice(h * P, (h + 1) * P)
                link(v.tensor_tensor(xT_lo[:, :, own], G0[:, h * D:(h + 1) * D].rearrange("p (c n) -> p c n", n=P),
                                     xT_hi[:, :, own].bitcast(F32), ALU.subtract))
                stage(f"x1T{h}")
            lows(END["upd"] + NB, END["h1"])

            dve.wait_ge(biases_in, 80)
            for h, k in ((0, 0), (0, 1), (1, 0), (1, 1)):
                dve.wait_ge(act_step, act_at(f"h1_{h}"))
                link(v.scalar_tensor_tensor(y1[:, h, :], h1[:, h, :], 1.0, bias_bc[:, k, :],
                                            ALU.mult, ALU.mult, accum_out=small[:, 12 + 2 * k + h:13 + 2 * k + h]))
                if k == 0:
                    link(v.tensor_scalar(y2[:, 0, h * P:(h + 1) * P], ident[:], small[:, 12 + h:13 + h], None,
                                         ALU.mult))
                if (h, k) == (1, 0):
                    stage("al")
            dve.wait_ge(pe_step, pe_at("albc"))
            for h in range(2):
                link(v.tensor_scalar(PT[:, h, :], G0[:, 0:N], small[:, 14 + h:15 + h], None, ALU.add))
            link(v.scalar_tensor_tensor(PT[:], PT[:], SLOPE, PT[:], ALU.mult, ALU.max))
            stage("lr")
            dve.wait_ge(act_step, act_at("lrelu"))
            link(v.tensor_tensor(PT[:], PT[:], S_cnt[:, 0, :, :], ALU.mult))
            stage("ET")
            dve.wait_ge(pe_step, pe_at("hp0"))
            link(v.tensor_scalar(small[:, 4:6], G0[:, 512:1024].rearrange("p (h n) -> p h n", h=2)[:, :, 0],
                                 EPS_L1, None, ALU.add))
            link(v.reciprocal(small[:, 6:8], small[:, 4:6]))
            for h in range(2):
                dve.wait_ge(pe_step, pe_at(f"hp{h}"))
                link(v.tensor_scalar(y2[:, h, :], G1[:, h * D:(h + 1) * D], small[:, 6 + h:7 + h], 0.0, ALU.mult,
                                     ALU.min))
                stage(f"neg{h}")
            for h in range(2):
                dve.wait_ge(act_step, act_at(f"elu{h}"))
                dve.wait_ge(with_x1, h + 1)
                link(v.scalar_tensor_tensor(y1[:, h, :], y2[:, h, :], -1.0, y1[:, h, :], ALU.add, ALU.add))
                if h == 1:
                    first_half_scale("sd2")
                    stage("scale2")
                statistics(h)
                stage(f"var{2 + h}")
            normalise_second_half(y2[:, 1, :], "sd3")
            stage("out1")

        @block.tensor
        def _(pe):
            mm = nc.tensor.matmul
            said = [0]

            def stage(ins, name):
                assert PE_STAGES[said[0]] == name, name
                said[0] += 1
                ins.then_inc(pe_step, 1)

            def split_chunk(n):
                pe.wait_ge(lo_pool if by_pool(n) else lo_made, lo_count(n, by_pool(n)))
                return W_hi[:, n % NB, :], W_lo[:, n % NB, :]

            def dense(a, b, acc, hi, lo, blocks, first, end):
                for n in range(a, b):
                    W1, W0 = split_chunk(n)
                    for m in range(blocks):
                        for x_part, W_parts in ((hi, (W1, W0)), (lo, (W1,))):
                            for f in range(0, D, 512):
                                for W in W_parts:
                                    ins = mm(acc[:, m * D + f:m * D + f + 512], x_part(n - first, m), W[:, f:f + 512],
                                             start=(n == first and x_part is hi and W is W1),
                                             stop=(n == end - 1 and x_part is lo))
                    ins.then_inc(chunk_used, 1)

            def x_dense(a, b, acc, first=None, end=None):
                dense(a, b, acc, lambda c, m: xT_hi[:, c, m * P:(m + 1) * P],
                      lambda c, m: xT_lo[:, c, m * P:(m + 1) * P], 2, a if first is None else first,
                      b if end is None else end)

            def block_by_block(g, acc, first, features, first_block):
                for m in range(2):
                    if features:
                        pe.wait_ge(dve_step, dve_at(f"{features}{m}"))
                    for n in range(g, g + NB):
                        W1, W0 = split_chunk(n)
                        c, nodes = n - first, slice(m * P, (m + 1) * P)
                        for part, Ws in ((xT_hi, (W1, W0)), (xT_lo, (W1,))):
                            for f in range(0, D, 512):
                                for W in Ws:
                                    ins = mm(acc[:, m * D + f:m * D + f + 512], part[:, c, nodes], W[:, f:f + 512],
                                             start=(c == 0 and part is xT_hi and W is W1),
                                             stop=(c == KC - 1 and part is xT_lo))
                        if m == 1:
                            ins.then_inc(chunk_used, 1)
                    if m == 0 and first_block:
                        stage(ins, first_block)

            def open_bank(b):
                mm(bank(b), zero_b[0:1, 0:P], zero_b[0:1, :], start=True, stop=False, skip_group_check=True)

            pe.wait_ge(x_in, 16)
            pe.wait_ge(setup_done, 1)
            for c in range(KC):
                for h in range(2):
                    ins = nc.tensor.transpose(G0[:, c * N + h * P:c * N + (h + 1) * P], x_nat[:, h, c * P:(c + 1) * P],
                                              ident[:])
            stage(ins, "xT")
            for k in range(2):
                pe.wait_ge(st_oh, 2 * k + 2)
                for c in range(KC):
                    for h in range(2):
                        ins = mm(G1[:, (k * KC + c) * P:(k * KC + c + 1) * P], x_nat[:, h, c * P:(c + 1) * P],
                                 st_ohT[:, k, h, :], start=(h == 0), stop=(h == 1))
                stage(ins, f"ghT{k}")
            pe.wait_ge(dve_step, dve_at("xT"))
            mm(bank(2)[:, 0:NC], tri[:], tot[:], start=True, stop=True)
            stage(mm(bank(2)[:, NC:2 * NC], ones_b[:], tot[:], start=True, stop=True), "totals")
            for k in range(2):
                pe.wait_ge(dve_step, dve_at(f"ghT{k}"))
                dense(k * KC, (k + 1) * KC, G0, lambda c, m: hh_hi[:, k, c % KC, :],
                      lambda c, m: hh_lo[:, k, c % KC, :], 1, 0, END["hh"])

            def scatter_static(t):
                logits, counts = (bank(2), bank(3)) if t == 0 else (bank(0), bank(1))
                pe.wait_ge(st_made, t + 1)
                for h in range(2):
                    for r in range(3):
                        mm(logits[:, h * N:(h + 1) * N], st_scl[:, h * P:(h + 1) * P], st_scr[:, r, :],
                           start=(t <= 1 and h == 0 and r == 0), stop=(t in (0, JO) and r == 2), skip_group_check=True)
                    ins = mm(counts[:, h * N:(h + 1) * N], st_scl[:, h * P:(h + 1) * P], st_one[:],
                             start=(t <= 1 and h == 0), stop=t in (0, JO), skip_group_check=True)
                ins.then_inc(scattered, 1)

            x_dense(END["hh"], END["hh"] + 4, G1, END["hh"], END["ooA"])
            pe.wait_ge(dve_step, dve_at("slots"))
            scatter_static(0)
            x_dense(END["hh"] + 4, END["ooA"], G1, END["hh"], END["ooA"])
            pe.wait_ge(dve_step, dve_at("D_hh"))
            x_dense(END["ooA"], END["ooB"], G0)

            def perm(s, dest):
                pe.wait_ge(placed, s + 1)

                for j in range(JS):
                    ins = mm(dest[:, 0:2 * NT], pos_oh[:, j, :], tile_val[:, j, :, :].rearrange("p k t -> p (k t)"),
                             start=(j == 0), stop=(j == JS - 1))
                stage(ins, f"perm{s}")

            pe.wait_ge(dve_step, dve_at("ooA_lo"))
            perm(0, bank(4))
            pe.wait_ge(dve_step, dve_at("ooB_lo"))
            for t in range(1, JO + 1):
                acc = G1[:, (t % 2) * D:(t % 2 + 1) * D]
                pe.wait_ge(st_oh, 4 + 4 * t)
                if t == 2:
                    pe.wait_ge(dve_step, dve_at("key0"))
                if t >= 3:
                    pe.wait_ge(reduced, t - 1)
                for i, (k, h, part) in enumerate((k, h, part) for k in range(2) for h in range(2) for part in range(2)):
                    tab = (Ao_tab, Bo_tab)[k]
                    for n in range(2):
                        ins = mm(acc[:, n * 512:(n + 1) * 512], st_ohTr[:, t % 2, k, h, :],
                                 tab[:, h, part, n * 512:(n + 1) * 512], start=(i == 0), stop=(i == 7))
                ins.then_inc(gathered, 1)
            pe.wait_ge(reduced, 1 + JO)
            for n in range(END["ooB"], END["hoA"]):
                x_dense(n, n + 1, G1, END["ooB"], END["hoA"])
                t = n - END["ooB"] - 1
                if 1 <= t <= JO:
                    scatter_static(t)
            perm(1, bank(3))
            pe.wait_ge(dve_step, dve_at("keys"))
            x_dense(END["hoA"], END["hoA"] + 3, G0, END["hoA"], END["hoB"])
            pe.wait_ge(dve_step, dve_at("hoA_lo"))
            for k in range(2):
                ins = nc.tensor.transpose(bank(4)[0:NT, k * P:(k + 1) * P], key_col[:, k, :], ident[:])
            stage(ins, "keysT")
            x_dense(END["hoA"] + 3, END["hoA"] + NB, G0, END["hoA"], END["hoB"])
            block_by_block(END["hoA"] + NB, G0, END["hoA"], None, "hoB_0")
            pe.wait_ge(dve_step, dve_at("hoB_lo"))

            open_bank(0)
            open_bank(1)

            def load(t):
                row = steer[0:1, t, :] if isinstance(t, int) else \
                    steer[0:1, bass.ds(t, 1), :].rearrange("p t c -> p (t c)")
                return nc.values_load_multi_w_load_instructions(
                    row, engines=(mybir.EngineType.PE,), min_val=0, max_val=3 * D,
                    skip_runtime_bounds_check_because="columns by their making")[1]

            def gather(t, b, sq, dq):
                pe.wait_ge(oh_made, t + 1)
                if not isinstance(t, int):
                    pe.wait_ge(reduced, 1 + JO + t - 1)
                elif t >= 2:
                    pe.wait_ge(reduced, 1 + JO + t - 1)
                for k, (tab, q) in enumerate(((A_tab, sq), (B_tab, dq))):
                    for n in range(2):
                        ins = mm(G1[:, (b % 2) * D + n * 512:(b % 2) * D + (n + 1) * 512], oh[:, b % 2, k, :],
                                 tab[:].rearrange("p q d -> p (q d)")[:, n * 512:][:, bass.ds(q, 512)],
                                 start=(k == 0), stop=(k == 1))
                ins.then_inc(gathered, 1)

            def scatter(t, b, column):
                pe.wait_ge(ones_made, t + 1)
                if isinstance(t, int) and t >= NT - U:
                    pe.wait_ge(last_made, t - (NT - U) + 1)
                else:
                    pe.wait_ge(sc_made, 2 * (t + 1))
                ins = mm(G0[:, bass.ds(column.with_bounds(min_val=0, max_val=14 * Q), 2 * Q)], sc_l[:, b, :],
                         sc_r[:, b, :, :].rearrange("p r n -> p (r n)"),
                         start=False, stop=False, skip_group_check=True)
                ins.then_inc(scattered, 1)

            def ho_turn(i):
                for b in range(U):
                    of_source, of_target, column = load(U * i + b)
                    gather(U * i + b, b, of_source, of_target)
                    if not isinstance(i, int) or U * i + b >= LAG:
                        scatter(U * i + b - LAG, (b - LAG) % U, column)

            peeled = 2 + TURNS % 2
            for i in range(peeled):
                ho_turn(i)
            with pe.Fori(0, (TURNS - peeled) // 2) as i:
                ho_turn(2 * i + peeled)
                ho_turn(2 * i + peeled + 1)
            for t in range(NT - LAG, NT - U):
                scatter(t, t % U, load(t + LAG)[2])

            def update(a, b):
                for n in range(a, b):
                    name, k = chunks[n]
                    (hi, lo, both), c = ((xT_hi, xT_lo, x_both), (zT_hi, zT_lo, z_both))[k // KC], k % KC
                    W1, W0 = split_chunk(n)
                    first, final = k == 0, k == 2 * KC - 1
                    if n == END["hoB"] + 2:
                        pe.wait_ge(reduced, 1 + JO + NT)
                    q = 0 if name == "hn" else 1
                    acc = ps[:, (2 + 2 * q) * 512:(4 + 2 * q) * 512]
                    for f in range(0, D, 512):
                        for W in (W1, W0):
                            ins = mm(acc[:, f:f + 512], both[:, c, q, :, :].rearrange("p k n -> p (k n)"),
                                     W[:, f:f + 512], start=first and W is W1, stop=final and W is W0)
                    if n == END["upd"] - 1:
                        stage(ins, "q1")
                    if q == 1:
                        for part, Ws in ((hi, (W1, W0)), (lo, (W1,))):
                            for f in range(0, D, 512):
                                for W in Ws:
                                    ins = mm(G1[:, D + f:D + f + 512], part[:, c, P:N], W[:, f:f + 512],
                                             start=first and part is hi and W is W1, stop=final and part is lo)
                    ins.then_inc(chunk_used, 1)

            pe.wait_ge(both_made, 4)
            update(END["hoB"], END["hoB"] + 2)
            for t in range(NT - U, NT):
                scatter(t, t % U, load(t + LAG)[2])
            update(END["hoB"] + 2, UX)
            pe.wait_ge(dve_step, dve_at("P"))
            for hs in range(2):
                for hd in range(2):
                    ins = nc.tensor.transpose(bank(0)[:, hs * N + hd * P:hs * N + (hd + 1) * P],
                                              S_log[:, 0, hd, hs * P:(hs + 1) * P], ident[:])
            stage(ins, "PT")
            pe.wait_ge(dve_step, dve_at("PT"))
            for s in range(2):
                if s == 1:
                    pe.wait_ge(dve_step, dve_at("zT0"))
                for c in range(4):
                    for hs in range(2):
                        d = 4 * s + c
                        ins = mm(G0[:, c * N:(c + 1) * N], x_nat[:, hs, d * P:(d + 1) * P], PT[:, hs, :],
                                 start=(hs == 0), stop=(hs == 1))
                stage(ins, f"zT{s}")
                update(UX + 2 * s, UX + 2 * s + 2)
            update(UX + 4, END["updx"])
            pe.wait_ge(dve_step, dve_at("zT1"))
            update(END["updx"], END["upd"])
            for h in range(2):
                if h == 0:
                    pe.wait_ge(act_step, act_at("x1_0"))
                else:
                    pe.wait_ge(dve_step, dve_at("x1_1"))
                for c in range(KC):
                    ins = nc.tensor.transpose(G0[:, h * D + c * P:h * D + (c + 1) * P], x1[:, h, c * P:(c + 1) * P],
                                              ident[:])
                stage(ins, f"x1T{h}")
            for g in range(END["upd"], END["h1"], NB):
                block_by_block(g, G1, END["upd"], "x1T", "h_0" if g + NB == END["h1"] else None)
            pe.wait_ge(dve_step, dve_at("al"))
            stage(mm(G0[:, 0:N], ones_f[:], y2[:, 0, 0:N], start=True, stop=True), "albc")
            pe.wait_ge(dve_step, dve_at("ET"))
            for hs in range(2):
                for hd in range(2):
                    mm(G0[:, 512 + hs * N:512 + hs * N + 1], PT[:, hd, hs * P:(hs + 1) * P], ones_f[:, 0:1],
                       start=(hd == 0), stop=(hd == 1))
            for hs in range(2):
                for n in range(2):
                    for hd in range(2):
                        ins = mm(G1[:, hs * D + n * 512:hs * D + (n + 1) * 512], PT[:, hd, hs * P:(hs + 1) * P],
                                 h1[:, hd, n * 512:(n + 1) * 512], start=(hd == 0), stop=(hd == 1))
                stage(ins, f"hp{hs}")


_INS = ['x', 'src', 'dst', 'L0_gnn_W_hh', 'L0_gnn_b_hh', 'L0_gnn_W_oo', 'L0_gnn_b_oo', 'L0_gnn_W_ho', 'L0_gnn_b_ho',
        'L0_gnn_W_a', 'L0_gnn_b_a', 'L0_gnn_W_hn', 'L0_gnn_b_hn', 'L0_gnn_W_on', 'L0_gnn_b_on', 'L1_gnn_W', 'L1_gnn_a']


def kernel(**inputs):
    import numpy as _np
    import concourse.bacc as _bacc
    from concourse import mybir as _mybir
    from concourse.bass_utils import run_bass_kernel_spmd as _run

    nc = _bacc.Bacc("TRN2", target_bir_lowering=False, num_devices=1)
    arrays, args = {}, []
    for name in _INS:
        a = _np.ascontiguousarray(inputs[name])
        arrays[f"in_{name}_dram"] = a
        args.append(nc.dram_tensor(f"in_{name}_dram", a.shape, _mybir.dt.from_np(a.dtype), kind="ExternalInput").ap())
    args.append(nc.dram_tensor("out_0_dram", (N, D), F32, kind="ExternalOutput").ap())
    gnn_two_layers(nc, *args)
    r = _run(nc, [arrays], core_ids=[0])
    return r.results[0]["out_0_dram"]
```
